# Optimizing a Trainium2 kernel written in Bass

```python
import numpy as np
import jax
import jax.numpy as jnp

def _softmax(x, axis=-1):
    return jax.nn.softmax(x, axis=axis)

def _gelu(x):
    return jax.nn.gelu(x, approximate=True)

def _silu(x):
    return jax.nn.silu(x)

def _sigmoid(x):
    return jax.nn.sigmoid(x)

def _layernorm(x, axis=-1, eps=1e-05):
    m = jnp.mean(x, axis=axis, keepdims=True)
    v = jnp.var(x, axis=axis, keepdims=True)
    return (x - m) / jnp.sqrt(v + eps)

def _scatter_add(tgt, idx, src, axis=0):
    return tgt.at[idx].add(src)

def _segment_sum(src, seg, n):
    return jax.ops.segment_sum(src, seg, n)
kernel_name = 'mk_seq_preln_d1_jaxref_r4_f01435'

def setup_inputs(seed: int=0):
    np.random.seed(seed)
    _w = jnp.asarray

    def _L0_attn_setup():
        import jax, jax.numpy as jnp
        import numpy as np
        BLOCK_H = 32
        BLOCK_W = 32
        N_FEAT = 1024
        K_FEAT = 1024
        key = jax.random.key(seed)
        k1, k2, k3 = jax.random.split(key, 3)
        data = jax.random.normal(k1, (4, 256, K_FEAT), dtype=jnp.float32)
        weight = jax.random.normal(k2, (N_FEAT, K_FEAT), dtype=jnp.float32) * 0.02
        nb, kb = (N_FEAT // BLOCK_H, K_FEAT // BLOCK_W)
        block_pattern = jax.random.randint(k3, (nb, kb), 0, 2, dtype=jnp.int32)
        mask = jnp.repeat(jnp.repeat(block_pattern, BLOCK_H, axis=0), BLOCK_W, axis=1)
        return {'data': data, 'weight': weight, 'mask': mask}
    _L0_attn_in = _L0_attn_setup()

    def _L0_ffn_setup():
        import jax, jax.numpy as jnp
        import numpy as np
        TOP_K = 2
        key = jax.random.key(seed)
        k0, k1, k2 = jax.random.split(key, 3)
        B, S, D, H, E = (4, 512, 1024, 1024, 8)
        sc = 1.0 / np.sqrt(D).astype(np.float32)
        x = jax.random.normal(k0, (B, S, D), dtype=jnp.float32)
        W_gate = jax.random.normal(k1, (D, E), dtype=jnp.float32) * sc
        b_gate = jnp.zeros((E,), dtype=jnp.float32)
        W_e = jax.random.normal(k2, (E, D, H), dtype=jnp.float32) * sc
        b_e = jnp.zeros((E, H), dtype=jnp.float32)
        return {'x': x, 'W_gate': W_gate, 'b_gate': b_gate, 'W_e': W_e, 'b_e': b_e}
    _L0_ffn_in = _L0_ffn_setup()
    _d = {'L0_attn_data': _L0_attn_in['data'], 'L0_attn_weight': _L0_attn_in['weight'], 'L0_attn_mask': _L0_attn_in['mask'], 'L0_ffn_W_gate': _L0_ffn_in['W_gate'], 'L0_ffn_b_gate': _L0_ffn_in['b_gate'], 'L0_ffn_W_e': _L0_ffn_in['W_e'], 'L0_ffn_b_e': _L0_ffn_in['b_e']}
    _x0 = _d['L0_attn_data']
    _d['L0_attn_data'] = jax.random.normal(jax.random.fold_in(jax.random.key(seed), 1), (4, 512, 1024), dtype=_x0.dtype)
    del _x0
    return _d

def reference(L0_attn_data, L0_attn_weight, L0_attn_mask, L0_ffn_W_gate, L0_ffn_b_gate, L0_ffn_W_e, L0_ffn_b_e):

    def _L0_attn_ref(data, weight, mask):
        import jax, jax.numpy as jnp
        import numpy as np
        BLOCK_H = 32
        BLOCK_W = 32
        N_FEAT = 1024
        K_FEAT = 1024
        N, K = weight.shape
        nb, kb = (N // BLOCK_H, K // BLOCK_W)
        block_mask = mask.reshape(nb, BLOCK_H, kb, BLOCK_W).astype(jnp.float32).sum(axis=(1, 3)) > 0
        elem_mask = jnp.repeat(jnp.repeat(block_mask, BLOCK_H, axis=0), BLOCK_W, axis=1)
        w_masked = weight * elem_mask.astype(weight.dtype)
        out = jnp.einsum('bsk,nk->bsn', data, w_masked)
        return out

    def _L0_ffn_ref(x, W_gate, b_gate, W_e, b_e):
        import jax, jax.numpy as jnp
        import numpy as np
        TOP_K = 2
        logits = x @ W_gate + b_gate
        _, top_idx = jax.lax.top_k(logits, TOP_K)
        y_all = jax.nn.relu(jnp.einsum('bsd,edh->bseh', x, W_e) + b_e)
        y = jnp.take_along_axis(y_all, top_idx[..., None], axis=2)
        return y.mean(axis=2)
    x = L0_attn_data
    x = x + _L0_attn_ref(_layernorm(x, axis=-1), L0_attn_weight, L0_attn_mask)
    x = x + _L0_ffn_ref(_layernorm(x, axis=-1), L0_ffn_W_gate, L0_ffn_b_gate, L0_ffn_W_e, L0_ffn_b_e)
    return x

_drawn_inputs = setup_inputs


def setup_inputs(seed=0):
    import zlib

    import numpy as np

    out = dict(_drawn_inputs(seed))
    spreads = {'L0_ffn_b_gate': (0.0, 0.1), 'L0_ffn_b_e': (0.0, 0.1)}
    factors = {}
    for name, (base, spread) in spreads.items():
        noise = np.random.default_rng([zlib.crc32(name.encode()), seed]).standard_normal(out[name].shape)
        drawn = base * np.exp(spread * noise) if base else spread * noise
        out[name] = jnp.asarray(drawn.astype(out[name].dtype))
    for name, factor in factors.items():
        out[name] = (out[name] * factor).astype(out[name].dtype)
    return out
```

```python
from contextlib import ExitStack

import concourse.bass as bass
from concourse import mybir

F32 = mybir.dt.float32
F32R = mybir.dt.float32r
F16 = mybir.dt.float16
I32 = mybir.dt.int32
ALU = mybir.AluOpType
ACT = mybir.ActivationFunctionType
AX = mybir.AxisListType

P = 128
EPS = 1e-5
TOP_K = 2
HI, LO = 0, 1
GATHER, ADD = 0, 1
PASSES = [(HI, HI), (HI, LO), (LO, HI)]


class Chain:

    def __init__(self, sem, steps=1, base=0):
        self.sem, self.steps, self.base = sem, steps, base

    def done(self, instruction):
        instruction.then_inc(self.sem, 1)

    def wait(self, engine, block, step=None, alone=None):
        value = self.base + block * self.steps + (self.steps if step is None else step)
        if not isinstance(value, int) or value > 0:
            engine.wait_ge(self.sem, value)
            if alone is not None and not isinstance(value, int):
                engine.sem_inc(alone, 1)


class Landings:

    def __init__(self, sems):
        self.sems = sems

    def done(self, instruction, parity):
        instruction.then_inc(self.sems[parity], 16)

    def wait(self, engine, parity, half):
        value = 16 * half + 16
        if not isinstance(value, int) or value > 0:
            engine.wait_ge(self.sems[parity], value)


def pipeline(engine, stages, n):
    stages = [(s[0], s[1], s[2] if len(s) > 2 else 0) for s in stages]
    leads = [lead for _, lead, _ in stages]
    first, last = -max(leads), n - min(leads)
    start = -min(leads) + 2
    turns = (n - max(leads) - start) // 2

    def peeled(lo, hi):
        for i in range(lo, hi):
            for stage, lead, from_block in stages:
                b = i + lead
                if from_block <= b < n:
                    stage(b, b % 2, b // 2)

    if turns < 2:
        peeled(first, last)
        return
    peeled(first, start)
    with engine.Fori(0, turns) as j:
        for u in range(2):
            for stage, lead, _ in stages:
                base = start + u + lead
                stage(2 * j + base, base % 2, j + base // 2)
    peeled(start + 2 * turns, last)


def build(nc, data, weight, mask, w_gate, b_gate, w_e, b_e, out):
    N_TOK, D = data.shape
    N_EXP, _, H = w_e.shape
    KT = D // P
    NB = N_TOK // P
    HALF = 512
    NH = H // HALF
    SUB = 32
    NSUB = D // SUB
    JB = N_TOK // P
    NC = N_EXP * JB
    N_BLOCKS = (TOP_K * N_TOK + N_EXP * (P - 1)) // P
    assert D == 1024 and H == D and weight.shape == (D, D) and NC == P and N_EXP == 8
    HD = D // 2

    ctx = ExitStack()
    with ctx:
        split_rows = nc.dram_tensor("split_rows", (N_TOK, 2 * D), F32, kind="Internal").ap()
        split_bias = nc.dram_tensor("split_bias", (N_EXP, 2, H), F32, kind="Internal").ap()

        cursor = [(nc.sbuf_base + 63) // 64 * 64]

        def at(name, shape, dt, offset):
            return nc.alloc_sbuf_tensor_at(name, shape, dt, offset=offset)

        def sb(name, shape, dt):
            size = 1
            for s in shape[1:]:
                size *= s
            size *= 2 if dt == F16 else 4
            t = at(name, shape, dt, cursor[0])
            cursor[0] += (size + 31) // 32 * 32
            return t

        slot_base = cursor[0]
        slots = sb("slots", [P, 2, 2, KT, H], F32R)
        slot_bytes = 2 * KT * H * 4
        w_stage = at("w_stage", [P, 2, D], F32, slot_base)
        mask_stage = at("mask_stage", [P, 2, D], I32, slot_base + 2 * D * 4)
        bias_raw = at("bias_raw", [N_EXP, H], F32, slot_base + 4 * D * 4)
        bias_hl = at("bias_hl", [N_EXP, 2, H], F32R, slot_base + 5 * D * 4)
        wT = at("wT", [P, 2, KT, D], F32R, slot_base + slot_bytes)

        raw = sb("raw", [P, 2, H], F32)
        bias_slot = sb("bias_slot", [2, 2, H], F32R)
        xb = sb("xb", [P, 2, D], F32)
        xr = sb("xr", [P, 2, D], F32)
        xT = sb("xT", [P, 2, 2, KT, P], F32R)
        hl = sb("hl", [P, 2, 2, D], F32R)
        x2_offset = cursor[0]
        x2 = sb("x2", [P, D], F32)
        x2T = sb("x2T", [P, KT, P], F32)

        ident = sb("ident", [P, P], F32)
        group = sb("group", [P, P], F32)
        tri = sb("tri", [P, P], F16)
        ones16 = sb("ones16", [P, P], F16)
        ones_bias = sb("ones_bias", [2, P], F32R)
        lane = sb("lane", [P, P], F32)
        lane_first = sb("lane_first", [P, JB], F32)
        tri_e = sb("tri_e", [P, N_EXP, N_EXP], F32)
        upto = sb("upto", [P, N_EXP], F32)
        eminus = sb("eminus", [P, 2], F32)
        tok = sb("tok", [P, 1], F32)
        half_neg = sb("half_neg", [P, 1], F32)
        wg = sb("wg", [P, KT, N_EXP], F32)
        bg = sb("bg", [P, N_EXP], F32)
        st = sb("st", [P, 2, 2, 6], F32)
        mv = sb("mv", [P, 2, 2, 2], F32)
        rs = sb("rs", [P, 2, 2], F32)
        msum = sb("msum", [P, 2, NSUB], F32)
        emask = sb("emask", [P, NSUB], F32)
        logit = sb("logit", [P, N_EXP], F32)
        gt = sb("gt", [P, N_EXP, N_EXP], F32)
        eq = sb("eq", [P, N_EXP, N_EXP], F32)
        rank = sb("rank", [P, N_EXP], F32)
        chosen = sb("chosen", [P, N_EXP], F16)
        chosen_tok = sb("chosen_tok", [P, 2, N_EXP], F32)
        count = sb("count", [P, N_EXP], F32)
        pos = sb("pos", [P, N_EXP], F32)
        pos_i = sb("pos_i", [P, N_EXP], I32)
        pos_r = sb("pos_r", [P, N_EXP], I32)
        pos_j = sb("pos_j", [P, N_EXP], I32)
        row_hot = sb("row_hot", [P, N_EXP, P], F16)
        blk_hot = sb("blk_hot", [P, N_EXP, JB], F32)
        blk_tok = sb("blk_tok", [P, N_EXP, JB], F16)
        queue = sb("queue", [P, NC], F32)
        end, cursor[0] = cursor[0], x2_offset
        act_row = sb("act_row", [P, N_EXP, JB], F32)
        act_col = sb("act_col", [P, 2], F32)
        act_c16 = sb("act_c16", [P, 2], F16)
        queueT = sb("queueT", [P, P], F32)
        pick = sb("pick", [P, N_BLOCKS], F32)
        meta_in = sb("meta_in", [P, N_BLOCKS + N_EXP], F16)
        empty = sb("empty", [P, N_BLOCKS], F32)
        tok_of = sb("tok_of", [P, N_BLOCKS], I32)
        tok_at = sb("tok_at", [P, 2, 2], I32)
        e_of = sb("e_of", [P, N_BLOCKS], I32)
        slot_of = sb("slot_of", [P, N_BLOCKS], I32)
        ready_of = sb("ready_of", [P, N_BLOCKS], I32)
        through = sb("through", [P, N_EXP], I32)
        assert cursor[0] <= x2_offset + D * 4 and end <= nc.sbuf_usable_end

        def ps(name, shape, dt=F32):
            return ctx.enter_context(nc.psum_tensor(name, shape, dt))

        psT = ps("psT", [P, 2, KT, P])
        psO = ps("psO", [P, NH, HALF])
        psG = ps("psG", [P, HALF])
        psN = ps("psN", [P, 2, N_EXP])
        psQ = psT[:, 1, 0, :]

        def sem(name):
            return ctx.enter_context(nc.semaphore(name))

        def chain(name, steps=1):
            return Chain(sem(name), steps)

        def landings(name):
            return Landings([sem(name + "_even"), sem(name + "_odd")])

        s_void = sem("s_void")
        s_const, s_vconst, s_small = sem("s_const"), chain("s_vconst"), sem("s_small")
        c_bsplit, s_bstore = chain("c_bsplit"), sem("s_bstore")
        l_w, l_m, l_x, l_xr, l_raw, l_bias = (landings(n) for n in ("l_w", "l_m", "l_x", "l_xr", "l_raw", "l_bias"))
        l_x1, l_split = landings("l_x1"), landings("l_split")
        l_gx, l_prev, l_scat = landings("l_gx"), landings("l_prev"), landings("l_scat")
        c_msum, c_wm, c_wlo, c_group, c_wt, c_whi = (chain("c_msum"), chain("c_wm", 2), chain("c_wlo"),
                                                     chain("c_group"), chain("c_wt"), chain("c_whi"))
        c_st1, c_ln1, c_t1, c_xhi, c_xlo = chain("c_st1", 3), chain("c_ln1", 3), chain("c_t1"), chain("c_xhi"), chain("c_xlo")
        c_mm, c_res, c_st2, c_ln2 = chain("c_mm", NH), chain("c_res", NH), chain("c_st2", 3), chain("c_ln2", 3)
        c_hi2, c_lo2, c_t2, c_x2T, c_gate = chain("c_hi2"), chain("c_lo2"), chain("c_t2"), chain("c_x2T"), chain("c_gate")
        c_top, c_pos, c_hot, c_ids, c_queue = chain("c_top", 9), chain("c_pos"), chain("c_hot", 8), chain("c_ids"), chain("c_queue")
        c_tab_d, c_tab_p = chain("c_tab_d"), chain("c_tab_p")
        c_split = chain("c_split", 2)
        c_tx, c_xT, c_half = chain("c_tx"), chain("c_xT"), Chain(sem("c_half"), NH, NH)
        c_tok = [chain("c_tok_gather"), chain("c_tok_add")]
        c_out, c_add = chain("c_out", NH), chain("c_add")

        block = ctx.enter_context(nc.Block())
        NCONST = 16

        @block.sync
        def _(eng):
            def load_w(r, p, h):
                c_wt.wait(eng, r - 2)
                l_w.done(eng.dma_start(w_stage[:, p, :], weight[bass.ds(r * P, P), :]), p)
                l_m.done(eng.dma_start(mask_stage[:, p, :], mask[bass.ds(r * P, P), :]), p)

            def load_x(t, p, h):
                c_t1.wait(eng, t - 2)
                l_x.done(eng.dma_start(xb[:, p, :], data[bass.ds(t * P, P), :]), p)

            def load_residual(t, p, h):
                l_x1.wait(eng, p, h - 1)
                c_ln2.wait(eng, t - 2)
                l_xr.done(eng.dma_start(xr[:, p, :], data[bass.ds(t * P, P), :]), p)

            def store_x1(t, p, h):
                c_res.wait(eng, t)
                l_x1.done(eng.dma_start(out[bass.ds(t * P, P), :], xr[:, p, :]), p)

            def store_split(t, p, h):
                c_hi2.wait(eng, t)
                c_lo2.wait(eng, t)
                l_split.done(eng.dma_start(split_rows[bass.ds(t * P, P), :].rearrange("p (a d) -> p a d", a=2),
                                           hl[:, p, :, :].bitcast(F32)), p)

            def load_chunk(e, kt, q):
                c_split.wait(eng, 2 * q + kt % 2 - 2)
                l_raw.done(eng.dma_start(raw[:, kt % 2, :], w_e[bass.ds(e, 1), kt * P:(kt + 1) * P, :]
                                         .rearrange("e p h -> p (e h)")), kt % 2)

            def load_bias(e, s):
                l_bias.done(eng.dma_start(bias_slot[:, s, :].bitcast(F32),
                                          split_bias[bass.ds(e, 1), :, :].rearrange("e a h -> (e a) h")), s)

            load_x(0, 0, 0)
            load_x(1, 1, 0)
            pipeline(eng, [(load_w, 0)], D // P)
            c_bsplit.wait(eng, 1)
            eng.dma_start(split_bias, bias_hl[:, :, :].bitcast(F32)).then_inc(s_bstore, 16)
            eng.wait_ge(s_bstore, 16)

            pipeline(eng, [(load_x, 3, 2),
                           (load_residual, 0), (store_x1, -1), (store_split, -1)], NB)
            for kt in range(KT):
                load_chunk(0, kt, kt // 2)
            load_bias(0, 0)
            for kt in range(KT):
                load_chunk(1, kt, KT // 2 + kt // 2)
            load_bias(1, 1)
            with eng.Fori(1, N_EXP // 2) as g:
                for s in range(2):
                    for kt in range(KT):
                        load_chunk(2 * g + s, kt, KT * g + s * KT // 2 + kt // 2)
                    load_bias(2 * g + s, s)

        @block.tensor
        def _(eng):
            def products(psum, p, moving, before_last=None):
                n = 0
                for a, b in PASSES:
                    for kt in range(KT):
                        last = eng.matmul(psum, xT[:, p, a, kt, :], moving(b, kt),
                                          start=(n == 0), stop=(n == len(PASSES) * KT - 1 and before_last is None))
                        n += 1
                if before_last is not None:
                    last = before_last()
                return last

            def group_sums(r, p, h):
                c_msum.wait(eng, r)
                c_wm.wait(eng, r - 1, 1)
                c_group.done(eng.matmul(psG[:, 0:NSUB], group[:], msum[:, p, :], start=True, stop=True))

            def transpose_w(r, p, h):
                c_wm.wait(eng, r)
                c_whi.wait(eng, r - 1)
                c_wlo.wait(eng, r - 1)
                for kt in range(KT):
                    last = eng.transpose(psT[:, 0, kt, :], w_stage[:, p, kt * P:(kt + 1) * P], ident[:])
                c_wt.done(last)

            def transpose_x(t, p, h):
                c_ln1.wait(eng, t)
                c_xhi.wait(eng, t - 1)
                c_xlo.wait(eng, t - 1)
                for kt in range(KT):
                    last = eng.transpose(psT[:, 0, kt, :], xb[:, p, kt * P:(kt + 1) * P], ident[:])
                c_t1.done(last)

            def project(t, p, h):
                c_xhi.wait(eng, t)
                c_xlo.wait(eng, t)
                for n in range(NH):
                    c_res.wait(eng, t - 1, n + 1)
                    c_mm.done(products(psO[:, n, :], p, lambda part, kt: wT[:, part, kt, n * HALF:(n + 1) * HALF]))

            def transpose_x2(t, p, h):
                c_ln2.wait(eng, t)
                c_x2T.wait(eng, t - 1)
                c_queue.wait(eng, t - 3)
                for kt in range(KT):
                    last = eng.transpose(psT[:, 1, kt, :], x2[:, kt * P:(kt + 1) * P], ident[:])
                c_t2.done(last)

            def gate(t, p, h):
                c_x2T.wait(eng, t)
                c_top.wait(eng, t - 1, 1)
                for kt in range(KT):
                    last = eng.matmul(psG[:, 0:N_EXP], x2T[:, kt, :], wg[:, kt, :], start=(kt == 0), stop=(kt == KT - 1))
                c_gate.done(last)

            def places(t, p, h):
                c_top.wait(eng, t)
                c_hot.wait(eng, t - 1, 2)
                eng.matmul(psN[:, 0, :], tri[:], chosen[:], start=True, stop=True)
                c_pos.done(eng.matmul(psN[:, 1, :], ones16[:], chosen[:], start=True, stop=True))

            def enqueue(t, p, h):
                c_hot.wait(eng, t)
                c_queue.wait(eng, t - 1)
                for e in range(N_EXP):
                    last = eng.matmul(psQ[:, e * JB:(e + 1) * JB], row_hot[:, e, :], blk_tok[:, e, :], start=True, stop=True)
                c_ids.done(last)

            eng.wait_ge(s_const, NCONST)
            pipeline(eng, [(group_sums, 1), (transpose_w, 0)], D // P)
            eng.wait_ge(s_small, 48)
            c_whi.wait(eng, D // P - 1)
            c_wlo.wait(eng, D // P - 1)
            transpose_x(0, 0, 0)
            pipeline(eng, [(transpose_x, 1, 1),
                           (project, 0), (transpose_x2, -1), (gate, -1), (places, -2), (enqueue, -3)], NB)

            c_tab_d.wait(eng, 0, 1)
            eng.transpose(psT[:, 0, 0, :], queue[:], ident[:])
            c_tab_p.done(eng.matmul(psG[:, 0:1], act_row[:].rearrange("p e j -> p (e j)"), ident[:, 0:1], start=True, stop=True))
            c_tab_d.wait(eng, 0, 3)
            c_tab_p.done(eng.matmul(psG[:, 16:17], tri[:], act_c16[:, 0:1], start=True, stop=True))
            c_tab_d.wait(eng, 0, 8)
            eng.matmul(psG[:, 64:64 + N_BLOCKS], queueT[:], pick[:], start=True, stop=True).then_inc(c_half.sem, NH)
            c_tab_p.done(eng.matmul(psG[:, 128:128 + N_BLOCKS + N_EXP], ones16[:], meta_in[:], start=True, stop=True))

            def transpose_rows(b, p, h):
                l_gx.wait(eng, p, h)
                c_xT.wait(eng, b - 1)
                for a in range(2):
                    for kt in range(KT):
                        last = eng.transpose(psT[:, a, kt, :], hl[:, p, a, kt * P:(kt + 1) * P].bitcast(F32), ident[:])
                c_tx.done(last)

            def expert(b, p, h):
                s = eng.value_load(slot_of[0:1, bass.ds(b, 1)], min_val=0, max_val=1)
                ready = eng.value_load(ready_of[0:1, bass.ds(b, 1)], min_val=2 * KT, max_val=2 * KT * N_EXP)
                c_xT.wait(eng, b)
                eng.wait_ge(c_split.sem, ready)
                for n in range(NH):
                    cols = slice(n * HALF, (n + 1) * HALF)
                    c_out.wait(eng, b - 1, n + 1)
                    moving = lambda part, kt: slots[:, bass.ds(s, 1), part, kt, cols].rearrange("p a n -> p (a n)")
                    bias = lambda: eng.matmul(psO[:, n, :], ones_bias[:, :],
                                              bias_slot[:, bass.ds(s, 1), cols].rearrange("p a n -> p (a n)"),
                                              start=False, stop=True)
                    c_half.done(products(psO[:, n, :], p, moving, bias))

            c_tab_d.wait(eng, 0, 14)
            pipeline(eng, [(transpose_rows, 1), (expert, 0)], N_BLOCKS)

        @block.scalar
        def _(eng):
            eng.dma_start(bias_raw[:], b_e).then_inc(s_small, 16)
            eng.dma_start(wg[:], w_gate.rearrange("(k p) e -> p k e", p=P)).then_inc(s_small, 16)
            eng.dma_start(bg[:], b_gate.partition_broadcast(P)).then_inc(s_small, 16)

            def w_hi(r, p, h):
                c_wt.wait(eng, r)
                c_whi.done(eng.activation(wT[:, HI, :, bass.ds(r * P, P)], psT[:, 0, :, :], ACT.Copy))

            def x_hi(t, p, h):
                c_t1.wait(eng, t)
                c_mm.wait(eng, t - 2)
                c_xhi.done(eng.activation(xT[:, p, HI, :, :], psT[:, 0, :, :], ACT.Copy))

            def x2_hi(t, p, h):
                c_ln2.wait(eng, t)
                l_split.wait(eng, p, h - 1)
                c_hi2.done(eng.activation(hl[:, p, HI, :], x2[:], ACT.Copy))

            def x2_columns(t, p, h):
                c_t2.wait(eng, t)
                c_gate.wait(eng, t - 1)
                c_x2T.done(eng.activation(x2T[:], psT[:, 1, :, :], ACT.Copy))

            pipeline(eng, [(w_hi, 0)], D // P)
            pipeline(eng, [(x_hi, 1), (x2_hi, -1), (x2_columns, -1)], NB)

            def rows_columns(b, p, h):
                c_tx.wait(eng, b)
                c_half.wait(eng, b - 2)
                c_xT.done(eng.activation(xT[:, p, :, :, :], psT[:], ACT.Copy))

            def relu_half(b, p, h):
                l_scat.wait(eng, p, h - 1)
                for n in range(NH):
                    c_half.wait(eng, b, n + 1)
                    c_out.done(eng.activation(xb[:, p, n * HALF:(n + 1) * HALF], psO[:, n, :], ACT.Relu, scale=1.0 / TOP_K))

            c_mm.wait(eng, NB - 1)
            pipeline(eng, [(rows_columns, 1), (relu_half, 0)], N_BLOCKS)

        @block.vector
        def _(eng):
            eng.wait_ge(s_const, NCONST)
            s_vconst.done(eng.tensor_copy(ones_bias[:], ones16[0:2, :]))
            s_vconst.done(eng.memset(count[:], 0.0))
            s_vconst.done(eng.memset(queue[:], 0.0))
            s_vconst.done(eng.tensor_reduce(eminus[:, 0:1], upto[:], AX.X, ALU.add))
            s_vconst.wait(eng, 3)
            s_vconst.done(eng.tensor_scalar(eminus[:, 1:2], eminus[:, 0:1], -1.0, 1.0, ALU.mult, ALU.add))

            def stats(c, src, which, t, p, landed):
                landed()
                c.wait(eng, t - 1)
                for g in range(2):
                    c.done(eng.bn_stats(st[:, which, g, :], src[:, g * HD:(g + 1) * HD]))
                c.wait(eng, t, 2, alone=s_void)
                c.done(eng.bn_aggr(mv[:, which, p, :], st[:, which, :, :].rearrange("p g s -> p (g s)")))

            def stats1(t, p, h):
                def landed():
                    l_x.wait(eng, p, h)
                    c_ln1.wait(eng, t - 2)
                stats(c_st1, xb[:, p, :], 0, t, p, landed)

            def stats2(t, p, h):
                def landed():
                    c_res.wait(eng, t)
                    c_ln2.wait(eng, t - 2)
                stats(c_st2, xr[:, p, :], 1, t, p, landed)

            def mask_sums(r, p, h):
                l_m.wait(eng, p, h)
                c_group.wait(eng, r - 2)
                c_msum.done(eng.tensor_reduce(msum[:, p, :], mask_stage[:, p, :].rearrange("p (g s) -> p g s", s=SUB),
                                              AX.X, ALU.add))

            def mask_w(r, p, h):
                c_group.wait(eng, r)
                c_wm.wait(eng, r - 1)
                c_wm.done(eng.tensor_scalar(emask[:], psG[:, 0:NSUB], 0.0, None, ALU.is_gt))
                l_w.wait(eng, p, h)
                c_wm.wait(eng, r, 1)
                rows = w_stage[:, p, :].rearrange("p (g s) -> p g s", s=SUB)
                c_wm.done(eng.tensor_tensor(rows, rows, emask[:].unsqueeze(2).to_broadcast([P, NSUB, SUB]), ALU.mult))

            def w_lo(r, p, h):
                c_whi.wait(eng, r)
                here = bass.ds(r * P, P)
                c_wlo.done(eng.tensor_tensor(wT[:, LO, :, here], psT[:, 0, :, :], wT[:, HI, :, here].bitcast(F32), ALU.subtract))

            def x_lo(t, p, h):
                c_xhi.wait(eng, t)
                c_xlo.done(eng.tensor_tensor(xT[:, p, LO, :, :], psT[:, 0, :, :], xT[:, p, HI, :, :].bitcast(F32), ALU.subtract))

            def residual(t, p, h):
                l_xr.wait(eng, p, h)
                for n in range(NH):
                    c_mm.wait(eng, t, n + 1)
                    cols = slice(n * HALF, (n + 1) * HALF)
                    c_res.done(eng.tensor_tensor(xr[:, p, cols], xr[:, p, cols], psO[:, n, :], ALU.add))

            def top2(t, p, h):
                c_gate.wait(eng, t)
                c_pos.wait(eng, t - 1)
                c_hot.wait(eng, t - 2)
                c_top.wait(eng, t - 1)
                mine = logit[:].unsqueeze(2).to_broadcast([P, N_EXP, N_EXP])
                other = logit[:].unsqueeze(1).to_broadcast([P, N_EXP, N_EXP])
                c_top.done(eng.tensor_tensor(logit[:], psG[:, 0:N_EXP], bg[:], ALU.add))
                c_top.wait(eng, t, 1)
                c_top.done(eng.tensor_tensor(eq[:], other, mine, ALU.is_equal))
                c_top.done(eng.tensor_tensor(gt[:], other, mine, ALU.is_gt))
                c_top.wait(eng, t, 2)
                c_top.done(eng.tensor_tensor(eq[:], eq[:], tri_e[:], ALU.mult))
                c_top.wait(eng, t, 4)
                c_top.done(eng.tensor_tensor(gt[:], gt[:], eq[:], ALU.add))
                c_top.wait(eng, t, 5)
                c_top.done(eng.tensor_reduce(rank[:], gt[:], AX.X, ALU.add))
                c_top.wait(eng, t, 6)
                c_top.done(eng.tensor_scalar(chosen_tok[:, p, :], rank[:], float(TOP_K), tok[:, 0:1], ALU.is_lt, ALU.mult))
                c_top.done(eng.tensor_scalar(chosen[:], rank[:], float(TOP_K), None, ALU.is_lt))
                c_top.wait(eng, t, 7)
                c_top.done(eng.tensor_scalar(tok[:], tok[:], float(P), None, ALU.add))

            def one_hots(t, p, h):
                c_pos.wait(eng, t)
                c_hot.wait(eng, t - 1)
                c_hot.done(eng.tensor_tensor(pos[:], psN[:, 0, :], count[:], ALU.add))
                c_hot.wait(eng, t, 1)
                c_hot.done(eng.tensor_tensor(count[:], count[:], psN[:, 1, :], ALU.add))
                c_hot.done(eng.tensor_copy(pos_i[:], pos[:]))
                c_hot.wait(eng, t, 3)
                c_hot.done(eng.tensor_scalar(pos_r[:], pos_i[:], P - 1, None, ALU.bitwise_and))
                c_hot.done(eng.tensor_scalar(pos_j[:], pos_i[:], P.bit_length() - 1, None, ALU.logical_shift_right))
                c_hot.wait(eng, t, 5)
                c_ids.wait(eng, t - 1)
                c_hot.done(eng.tensor_tensor(blk_hot[:], lane[:, 0:JB].unsqueeze(1).to_broadcast([P, N_EXP, JB]),
                                             pos_j[:].unsqueeze(2).to_broadcast([P, N_EXP, JB]), ALU.is_equal))
                c_hot.done(eng.tensor_tensor(row_hot[:], lane[:].unsqueeze(1).to_broadcast([P, N_EXP, P]),
                                             pos_r[:].unsqueeze(2).to_broadcast([P, N_EXP, P]), ALU.is_equal))
                c_hot.wait(eng, t, 6)
                c_hot.done(eng.tensor_tensor(blk_tok[:], blk_hot[:],
                                             chosen_tok[:, p, :].unsqueeze(2).to_broadcast([P, N_EXP, JB]), ALU.mult))

            def add_queue(t, p, h):
                c_ids.wait(eng, t)
                c_queue.wait(eng, t - 1)
                c_queue.done(eng.tensor_tensor(queue[:], queue[:], psQ, ALU.add))

            def split_chunk(e_slot, kt, q):
                l_raw.wait(eng, kt % 2, q)
                c = 2 * q + kt % 2
                c_split.done(eng.tensor_copy(slots[:, e_slot, HI, kt, :], raw[:, kt % 2, :]))
                c_split.wait(eng, c, 1)
                c_split.done(eng.tensor_tensor(slots[:, e_slot, LO, kt, :], raw[:, kt % 2, :],
                                               slots[:, e_slot, HI, kt, :].bitcast(F32), ALU.subtract))

            def split_expert(e_slot, e_half, q0):
                for kt in range(KT):
                    if kt == KT - 1:
                        l_bias.wait(eng, e_slot, e_half)
                    split_chunk(e_slot, kt, q0 + kt // 2)

            stats1(0, 0, 0)
            stats1(1, 1, 0)
            pipeline(eng, [(mask_sums, 1), (mask_w, 0), (w_lo, -1)], D // P)
            eng.wait_ge(s_small, 48)
            c_bsplit.done(eng.tensor_copy(bias_hl[:, HI, :], bias_raw[:]))
            c_bsplit.wait(eng, 0)
            c_bsplit.done(eng.tensor_tensor(bias_hl[:, LO, :], bias_raw[:], bias_hl[:, HI, :].bitcast(F32), ALU.subtract))
            pipeline(eng, [(residual, -1), (x_lo, 1), (stats2, -1),
                           (stats1, 2, 2),
                           (top2, -2), (one_hots, -3), (add_queue, -4)], NB)

            c_hot.wait(eng, NB - 1)
            c_queue.wait(eng, NB - 1)
            for used in (c_hi2, c_lo2, c_t2):
                used.wait(eng, NB - 1)
            tab = c_tab_d
            tab.done(eng.tensor_tensor(act_row[:], count[:].unsqueeze(2).to_broadcast([P, N_EXP, JB]),
                                       lane_first[:].unsqueeze(1).to_broadcast([P, N_EXP, JB]), ALU.is_gt))
            c_tab_p.wait(eng, 0, 1)
            tab.done(eng.tensor_copy(act_col[:, 0:1], psG[:, 0:1]))
            tab.done(eng.tensor_copy(act_c16[:, 0:1], psG[:, 0:1]))
            tab.done(eng.tensor_copy(queueT[:], psT[:, 0, 0, :]))
            c_tab_p.wait(eng, 0, 2)
            tab.done(eng.tensor_copy(act_col[:, 1:2], psG[:, 16:17]))
            tab.wait(eng, 0, 5)
            tab.done(eng.tensor_scalar(pick[:], lane[:, 0:N_BLOCKS], act_col[:, 1:2], act_col[:, 0:1], ALU.is_equal, ALU.mult))
            tab.done(eng.tensor_scalar(meta_in[:, N_BLOCKS:], upto[:], act_col[:, 0:1], None, ALU.mult))
            tab.wait(eng, 0, 6)
            tab.done(eng.tensor_scalar(meta_in[:, 0:N_BLOCKS], pick[:], eminus[:, 1:2], None, ALU.mult))
            c_tab_p.wait(eng, 0, 3)
            tab.done(eng.tensor_scalar(empty[:], psG[:, 64:64 + N_BLOCKS], 0.0, float(2 * N_TOK), ALU.is_equal, ALU.mult))
            tab.done(eng.tensor_scalar(e_of[:], psG[:, 128:128 + N_BLOCKS], float(N_EXP - 1), None, ALU.add))
            tab.done(eng.tensor_scalar(through[:], psG[:, 128 + N_BLOCKS:128 + N_BLOCKS + N_EXP], float(NH), float(NH), ALU.mult, ALU.add))
            tab.wait(eng, 0, 10)
            tab.done(eng.scalar_tensor_tensor(tok_of[:], psG[:, 64:64 + N_BLOCKS], -1.0, empty[:], ALU.add, ALU.add))
            tab.done(eng.tensor_scalar(slot_of[:], e_of[:], 1, None, ALU.bitwise_and))
            tab.done(eng.tensor_scalar(ready_of[:], e_of[:], 1.0, float(2 * KT), ALU.add, ALU.mult))

            eng.wait_ge(s_bstore, 16)
            split_expert(0, 0, 0)
            c_mm.wait(eng, NB - 1)
            split_expert(1, 0, KT // 2)
            tab.wait(eng, 0, 14)
            with eng.Fori(1, N_EXP // 2) as g:
                for s in range(2):
                    used = eng.value_load(through[0:1, bass.ds(2 * g + s - 2, 1)], min_val=NH, max_val=NH * (N_BLOCKS + 1))
                    eng.wait_ge(c_half.sem, used)
                    split_expert(s, g, KT * g + s * KT // 2)

        @block.gpsimd
        def _(eng):
            def const(instruction):
                instruction.then_inc(s_const, 1)

            const(eng.memset(ident[:], 0.0))
            const(eng.memset(group[:], 1.0))
            const(eng.memset(tri[:], 1.0))
            const(eng.memset(ones16[:], 1.0))
            const(eng.memset(tri_e[:], 1.0))
            const(eng.memset(upto[:], 1.0))
            const(eng.memset(half_neg[:], -0.5))
            const(eng.iota(lane[:], [[1, P]], base=0, channel_multiplier=0, allow_small_or_imprecise_dtypes=True))
            const(eng.iota(lane_first[:], [[P, JB]], base=0, channel_multiplier=0, allow_small_or_imprecise_dtypes=True))
            const(eng.iota(tok[:], [[0, 1]], base=1, channel_multiplier=1, allow_small_or_imprecise_dtypes=True))
            eng.wait_ge(s_const, 10)
            const(eng.affine_select(out=ident[:], in_=ident[:], pattern=[[-1, P]], compare_op=ALU.not_equal, fill=1.0,
                                    base=0, channel_multiplier=1))
            g4 = group[:].rearrange("p (g s) -> p g s", s=SUB)
            const(eng.affine_select(out=g4, in_=g4, pattern=[[-SUB, P // SUB], [0, SUB]], compare_op=ALU.is_ge, fill=0.0,
                                    base=0, channel_multiplier=1))
            const(eng.affine_select(out=tri[:], in_=tri[:], pattern=[[1, P]], compare_op=ALU.is_ge, fill=0.0,
                                    base=-1, channel_multiplier=-1))
            const(eng.affine_select(out=tri_e[:], in_=tri_e[:], pattern=[[1, N_EXP], [-1, N_EXP]], compare_op=ALU.is_ge,
                                    fill=0.0, base=-1, channel_multiplier=0))
            const(eng.affine_select(out=upto[:], in_=upto[:], pattern=[[JB, N_EXP]], compare_op=ALU.is_ge, fill=0.0,
                                    base=JB - 1, channel_multiplier=-1))
            eng.wait_ge(s_const, 15)
            const(eng.affine_select(out=g4, in_=g4, pattern=[[SUB, P // SUB], [0, SUB]], compare_op=ALU.is_ge, fill=0.0,
                                    base=SUB - 1, channel_multiplier=-1))

            def normalise(c, stats_done, which, src, dst, t, p):
                c.wait(eng, t - 1)
                stats_done.wait(eng, t, alone=s_void)
                c.done(eng.tensor_scalar(rs[:, which, 0:1], mv[:, which, p, 1:2], EPS, None, ALU.add))
                c.wait(eng, t, 1)
                c.done(eng.tensor_tensor(rs[:, which, 1:2], rs[:, which, 0:1], half_neg[:], ALU.pow))
                c.wait(eng, t, 2, alone=s_void)
                c.done(eng.tensor_scalar(dst, src, mv[:, which, p, 0:1], rs[:, which, 1:2], ALU.subtract, ALU.mult))

            def norm1(t, p, h):
                normalise(c_ln1, c_st1, 0, xb[:, p, :], xb[:, p, :], t, p)

            def norm2(t, p, h):
                c_t2.wait(eng, t - 1)
                c_hi2.wait(eng, t - 1)
                c_lo2.wait(eng, t - 1)
                normalise(c_ln2, c_st2, 1, xr[:, p, :], x2[:], t, p)

            def x2_lo(t, p, h):
                c_hi2.wait(eng, t)
                c_lo2.done(eng.tensor_tensor(hl[:, p, LO, :], x2[:], hl[:, p, HI, :].bitcast(F32), ALU.subtract))

            norm1(0, 0, 0)
            norm1(1, 1, 0)
            pipeline(eng, [(norm2, -1), (x2_lo, -1),
                           (norm1, 2, 2)], NB)

            def set_tokens(which, b, p):
                c_tok[which].done(eng.tensor_copy(tok_at[:, which, p:p + 1], tok_of[:, bass.ds(b, 1)]))
                c_tok[which].wait(eng, b, alone=s_void)

            def by_token(which, p):
                return bass.IndirectOffsetOnAxis(ap=tok_at[:, which, p:p + 1], axis=0)

            def gather_rows(b, p, h):
                c_tx.wait(eng, b - 2)
                set_tokens(GATHER, b, p)
                l_gx.done(eng.indirect_dma_start(hl[:, p, :, :].rearrange("p a d -> p (a d)").bitcast(F32), None,
                                                 split_rows, by_token(GATHER, p), bounds_check=N_TOK - 1, oob_is_err=False), p)

            def gather_so_far(b, p, h):
                if isinstance(b, int):
                    if b > 0:
                        l_scat.wait(eng, 1 - p, (b - 1) // 2)
                else:
                    l_scat.wait(eng, 1 - p, h if p == 1 else h - 1)
                c_add.wait(eng, b - 2)
                set_tokens(ADD, b, p)
                l_prev.done(eng.indirect_dma_start(xr[:, p, :], None, out, by_token(ADD, p), bounds_check=N_TOK - 1,
                                                   oob_is_err=False), p)

            def add_rows(b, p, h):
                l_prev.wait(eng, p, h)
                c_out.wait(eng, b)
                c_add.done(eng.tensor_tensor(xb[:, p, :], xb[:, p, :], xr[:, p, :], ALU.add))

            def scatter_rows(b, p, h):
                c_add.wait(eng, b, alone=s_void)
                l_scat.done(eng.indirect_dma_start(out, by_token(ADD, p), xb[:, p, :], None, bounds_check=N_TOK - 1,
                                                   oob_is_err=False), p)

            for p in range(2):
                l_x1.wait(eng, p, NB // 2 - 1)
                l_split.wait(eng, p, NB // 2 - 1)
            c_tab_d.wait(eng, 0, 12)
            pipeline(eng, [(gather_rows, 2), (gather_so_far, 0), (add_rows, 0), (scatter_rows, 0)], N_BLOCKS)
            for p in range(2):
                l_scat.wait(eng, p, (N_BLOCKS - 1 - p) // 2)


_INS = ["L0_attn_data", "L0_attn_weight", "L0_attn_mask", "L0_ffn_W_gate", "L0_ffn_b_gate", "L0_ffn_W_e", "L0_ffn_b_e"]


def kernel(**inputs):
    import numpy as np
    import concourse.bacc as bacc
    from concourse.bass_utils import run_bass_kernel_spmd

    nc = bacc.Bacc("TRN2", target_bir_lowering=False, num_devices=1)
    B, S, D = inputs["L0_attn_data"].shape
    arrays, args = {}, []
    for name in _INS:
        a = np.ascontiguousarray(inputs[name])
        if name == "L0_attn_data":
            a = a.reshape(B * S, D)
        arrays[name] = a
        args.append(nc.dram_tensor(name, a.shape, mybir.dt.from_np(a.dtype), kind="ExternalInput").ap())
    args.append(nc.dram_tensor("rows_out", (B * S, D), F32, kind="ExternalOutput").ap())
    build(nc, *args)
    r = run_bass_kernel_spmd(nc, [arrays], core_ids=[0])
    return r.results[0]["rows_out"].reshape(B, S, D)
```

```python
from contextlib import ExitStack

import concourse.bass as bass
from concourse import mybir

F32 = mybir.dt.float32
F32R = mybir.dt.float32r
F16 = mybir.dt.float16
I32 = mybir.dt.int32
ALU = mybir.AluOpType
ACT = mybir.ActivationFunctionType
AX = mybir.AxisListType

P = 128
EPS = 1e-5
TOP_K = 2
HI, LO = 0, 1
GATHER, ADD = 0, 1
PASSES = [(HI, HI), (HI, LO), (LO, HI)]


class Chain:

    def __init__(self, sem, steps=1, base=0):
        self.sem, self.steps, self.base = sem, steps, base

    def done(self, instruction):
        instruction.then_inc(self.sem, 1)

    def wait(self, engine, block, step=None, alone=None):
        value = self.base + block * self.steps + (self.steps if step is None else step)
        if not isinstance(value, int) or value > 0:
            engine.wait_ge(self.sem, value)
            if alone is not None and not isinstance(value, int):
                engine.sem_inc(alone, 1)


class Landings:

    def __init__(self, sems):
        self.sems = sems

    def done(self, instruction, parity):
        instruction.then_inc(self.sems[parity], 16)

    def wait(self, engine, parity, half):
        value = 16 * half + 16
        if not isinstance(value, int) or value > 0:
            engine.wait_ge(self.sems[parity], value)


def pipeline(engine, stages, n):
    stages = [(s[0], s[1], s[2] if len(s) > 2 else 0) for s in stages]
    leads = [lead for _, lead, _ in stages]
    first, last = -max(leads), n - min(leads)
    start = -min(leads) + 2
    turns = (n - max(leads) - start) // 2

    def peeled(lo, hi):
        for i in range(lo, hi):
            for stage, lead, from_block in stages:
                b = i + lead
                if from_block <= b < n:
                    stage(b, b % 2, b // 2)

    if turns < 2:
        peeled(first, last)
        return
    peeled(first, start)
    with engine.Fori(0, turns) as j:
        for u in range(2):
            for stage, lead, _ in stages:
                base = start + u + lead
                stage(2 * j + base, base % 2, j + base // 2)
    peeled(start + 2 * turns, last)


def build(nc, data, weight, mask, w_gate, b_gate, w_e, b_e, out):
    N_TOK, D = data.shape
    N_EXP, _, H = w_e.shape
    KT = D // P
    NB = N_TOK // P
    HALF = 512
    NH = H // HALF
    NT = D // P
    SUB = 32
    NSUB = D // SUB
    JB = N_TOK // P
    NC = N_EXP * JB
    N_BLOCKS = (TOP_K * N_TOK + N_EXP * (P - 1)) // P
    assert D == 1024 and H == D and weight.shape == (D, D) and NC == P and N_EXP == 8
    HD = D // 2

    ctx = ExitStack()
    with ctx:
        x2_rows = nc.dram_tensor("x2_rows", (N_TOK, D), F32, kind="Internal").ap()
        split_bias = nc.dram_tensor("split_bias", (N_EXP, 2, H), F32, kind="Internal").ap()

        cursor = [(nc.sbuf_base + 63) // 64 * 64]

        def at(name, shape, dt, offset):
            return nc.alloc_sbuf_tensor_at(name, shape, dt, offset=offset)

        def sb(name, shape, dt):
            size = 1
            for s in shape[1:]:
                size *= s
            size *= 2 if dt == F16 else 4
            t = at(name, shape, dt, cursor[0])
            cursor[0] += (size + 31) // 32 * 32
            return t

        slot_base = cursor[0]
        slots = sb("slots", [P, 2, 2, KT, H], F32R)
        slot_bytes = 2 * KT * H * 4
        w_stage = at("w_stage", [P, NT, D], F32, slot_base)
        mask_stage = at("mask_stage", [P, NT, D], I32, slot_base + NT * D * 4)
        wT = at("wT", [P, 2, KT, D], F32R, slot_base + slot_bytes)

        raw = sb("raw", [P, 2, H], F32)
        bias_slot = sb("bias_slot", [2, 2, H], F32R)
        xb = sb("xb", [P, 2, D], F32)
        xr_offset = cursor[0]
        xr = sb("xr", [P, 2, D], F32)
        xT = sb("xT", [P, 2, 2, KT, P], F32R)
        bias_hl = at("bias_hl", [N_EXP, 2, H], F32R, cursor[0])
        x2 = sb("x2", [P, 2, D], F32)
        bias_raw = at("bias_raw", [N_EXP, H], F32, cursor[0])
        x2T = sb("x2T", [P, KT, P], F32)

        ident = sb("ident", [P, P], F32)
        group = sb("group", [P, P], F32)
        msum = sb("msum", [P, NT, NSUB], F32)
        emask = sb("emask", [P, NT, NSUB], F32)
        tri = sb("tri", [P, P], F16)
        ones16 = sb("ones16", [P, P], F16)
        ones_bias = sb("ones_bias", [2, P], F32R)
        lane = sb("lane", [P, P], F16)
        lane_first = sb("lane_first", [P, JB], F32)
        tri_e = sb("tri_e", [P, N_EXP, N_EXP], F32)
        upto = sb("upto", [P, N_EXP], F32)
        eminus = sb("eminus", [P, 2], F32)
        tok = sb("tok", [P, 1], F32)
        spare = sb("spare", [P, 1], F32)
        half_neg = sb("half_neg", [P, 1], F32)
        wg = sb("wg", [P, KT, N_EXP], F32)
        bg = sb("bg", [P, N_EXP], F32)
        st = sb("st", [P, 2, 2, 6], F32)
        mv = sb("mv", [P, 2, 2, 2], F32)
        rs = sb("rs", [P, 2, 2], F32)
        logit = sb("logit", [P, N_EXP], F32)
        gt = sb("gt", [P, N_EXP, N_EXP], F32)
        eq = sb("eq", [P, N_EXP, N_EXP], F32)
        rank = sb("rank", [P, N_EXP], F32)
        chosen = sb("chosen", [P, N_EXP], F16)
        chosen_tok = sb("chosen_tok", [P, 2, N_EXP], F32)
        count = sb("count", [P, N_EXP], F32)
        pos = sb("pos", [P, N_EXP], F32)
        pos_i = sb("pos_i", [P, N_EXP], I32)
        pos_r = sb("pos_r", [P, N_EXP], I32)
        pos_j = sb("pos_j", [P, N_EXP], I32)
        row_hot = sb("row_hot", [P, N_EXP, P], F16)
        blk_hot = sb("blk_hot", [P, N_EXP, JB], F16)
        blk_tok = sb("blk_tok", [P, N_EXP, JB], F16)
        queue = sb("queue", [P, NC], F32)
        end, cursor[0] = cursor[0], xr_offset
        act_row = sb("act_row", [P, N_EXP, JB], F32)
        act_col = sb("act_col", [P, 2], F32)
        act_c16 = sb("act_c16", [P, 2], F16)
        queueT = sb("queueT", [P, P], F32)
        pick = sb("pick", [P, N_BLOCKS], F32)
        meta_in = sb("meta_in", [P, N_BLOCKS + N_EXP], F16)
        empty = sb("empty", [P, N_BLOCKS], F32)
        tok_of = sb("tok_of", [P, N_BLOCKS], I32)
        tok_at = sb("tok_at", [P, 2, 2], I32)
        e_of = sb("e_of", [P, N_BLOCKS], I32)
        slot_of = sb("slot_of", [P, N_BLOCKS], I32)
        ready_of = sb("ready_of", [P, N_BLOCKS], I32)
        through = sb("through", [P, N_EXP], I32)
        assert cursor[0] <= xr_offset + 2 * D * 4 and end <= nc.sbuf_usable_end

        def ps(name, shape, dt=F32):
            return ctx.enter_context(nc.psum_tensor(name, shape, dt))

        psT = ps("psT", [P, 2, KT, P])
        psO = ps("psO", [P, NH, HALF])
        psG = ps("psG", [P, HALF])
        psN = ps("psN", [P, 2, N_EXP])
        psQ = psT[:, 1, 0, :]

        def sem(name):
            return ctx.enter_context(nc.semaphore(name))

        def chain(name, steps=1):
            return Chain(sem(name), steps)

        def landings(name):
            return Landings([sem(name + "_even"), sem(name + "_odd")])

        s_void = sem("s_void")
        s_const, s_vconst, s_small = sem("s_const"), chain("s_vconst"), sem("s_small")
        c_bsplit, s_bstore = chain("c_bsplit"), sem("s_bstore")
        s_w = [sem(f"s_w{r}") for r in range(NT)]
        s_m = [sem(f"s_m{r}") for r in range(NT)]
        l_x, l_xr, l_raw, l_raw0, l_bias = (landings(n) for n in ("l_x", "l_xr", "l_raw", "l_raw0", "l_bias"))
        l_x1, l_x2 = landings("l_x1"), landings("l_x2")
        l_gather, l_add = landings("l_gather"), landings("l_add")
        s_spare = sem("s_spare")
        c_msum, c_em, c_wm, c_wlo = chain("c_msum"), chain("c_em"), chain("c_wm"), chain("c_wlo")
        c_group, c_wt, c_whi = chain("c_group"), chain("c_wt"), chain("c_whi")
        c_st1, c_ln1, c_t1, c_xhi, c_xlo = chain("c_st1", 3), chain("c_ln1"), chain("c_t1"), chain("c_xhi"), chain("c_xlo")
        c_mm, c_res, c_st2, c_ln2 = chain("c_mm", NH), chain("c_res", NH), chain("c_st2", 3), chain("c_ln2")
        c_rs = [chain("c_rs1", 2), chain("c_rs2", 2)]
        c_t2, c_x2T, c_gate = chain("c_t2"), chain("c_x2T"), chain("c_gate")
        c_top, c_pos, c_hot, c_ids, c_queue = chain("c_top", 9), chain("c_pos"), chain("c_hot", 8), chain("c_ids"), chain("c_queue")
        c_tab_d, c_tab_p = chain("c_tab_d"), chain("c_tab_p")
        c_hi0, c_lo0, c_split = chain("c_hi0"), chain("c_lo0"), chain("c_split", 2)
        c_turn, c_rhi, c_rlo, c_half = chain("c_turn"), chain("c_rhi", 2), chain("c_rlo"), Chain(sem("c_half"), NH, NH)
        c_tok = [chain("c_tok_gather"), chain("c_tok_add")]
        c_out = chain("c_out", NH)

        block = ctx.enter_context(nc.Block())
        NCONST = 18

        @block.sync
        def _(eng):
            def load_x(t, p, h):
                c_t1.wait(eng, t - 2)
                l_x.done(eng.dma_start(xb[:, p, :], data[bass.ds(t * P, P), :]), p)

            def load_residual(t, p, h):
                l_x1.wait(eng, p, h - 1)
                c_ln2.wait(eng, t - 2, alone=s_void)
                l_xr.done(eng.dma_start(xr[:, p, :], data[bass.ds(t * P, P), :]), p)

            def store_x1(t, p, h):
                c_res.wait(eng, t)
                l_x1.done(eng.dma_start(out[bass.ds(t * P, P), :], xr[:, p, :]), p)

            def store_x2(t, p, h):
                c_ln2.wait(eng, t)
                l_x2.done(eng.dma_start(x2_rows[bass.ds(t * P, P), :], x2[:, p, :]), p)

            def load_piece(t, p, h):
                c_lo0.wait(eng, t - 2, alone=s_void)
                l_raw0.done(eng.dma_start(raw[:, p, 0:HALF], w_e[0, bass.ds(h * P, P), p * HALF:(p + 1) * HALF]), p)

            def load_chunk(e, kt, q):
                c_split.wait(eng, KT + 2 * q + kt % 2 - 2)
                l_raw.done(eng.dma_start(raw[:, kt % 2, :], w_e[bass.ds(e, 1), kt * P:(kt + 1) * P, :]
                                         .rearrange("e p h -> p (e h)")), kt % 2)

            def load_bias(e, s):
                l_bias.done(eng.dma_start(bias_slot[:, s, :].bitcast(F32),
                                          split_bias[bass.ds(e, 1), :, :].rearrange("e a h -> (e a) h")), s)

            load_x(0, 0, 0)
            load_x(1, 1, 0)
            for r in range(NT):
                rows = slice(r * P, (r + 1) * P)
                eng.dma_start(mask_stage[:, r, :], mask[rows, :]).then_inc(s_m[r], 16)
                eng.dma_start(w_stage[:, r, :], weight[rows, :]).then_inc(s_w[r], 16)
            eng.wait_ge(s_const, NCONST)
            eng.dma_start(out[N_TOK:N_TOK + P, :], raw[:, 0, :]).then_inc(s_spare, 16)
            eng.wait_ge(s_spare, 16)
            c_bsplit.wait(eng, 1)
            eng.dma_start(split_bias, bias_hl[:, :, :].bitcast(F32)).then_inc(s_bstore, 16)
            pipeline(eng, [(load_residual, 0), (store_x1, -1), (load_piece, 0), (load_x, 3, 2), (store_x2, -1)], NB)
            eng.wait_ge(s_bstore, 16)
            load_bias(0, 0)
            for p in range(2):
                c_lo0.wait(eng, NB - 2 + p)
            for kt in range(KT):
                load_chunk(1, kt, kt // 2)
            load_bias(1, 1)
            with eng.Fori(1, N_EXP // 2) as g:
                for s in range(2):
                    for kt in range(KT):
                        load_chunk(2 * g + s, kt, KT * g + (s - 1) * KT // 2 + kt // 2)
                    load_bias(2 * g + s, s)

        @block.tensor
        def _(eng):
            def products(psum, p, moving, before_last=None):
                n = 0
                for a, b in PASSES:
                    for kt in range(KT):
                        last = eng.matmul(psum, xT[:, p, a, kt, :], moving(b, kt),
                                          start=(n == 0), stop=(n == len(PASSES) * KT - 1 and before_last is None))
                        n += 1
                if before_last is not None:
                    last = before_last()
                return last

            def group_sums(r):
                c_msum.wait(eng, r)
                c_em.wait(eng, r - 1)
                c_group.done(eng.matmul(psG[:, 0:NSUB], group[:], msum[:, r, :], start=True, stop=True))

            def transpose_w(r):
                c_wm.wait(eng, r)
                c_whi.wait(eng, r - 2)
                c_wlo.wait(eng, r - 2)
                for kt in range(KT):
                    last = eng.transpose(psT[:, r % 2, kt, :], w_stage[:, r, kt * P:(kt + 1) * P], ident[:])
                c_wt.done(last)

            def transpose_x(t, p, h):
                c_ln1.wait(eng, t)
                c_xlo.wait(eng, t - 1)
                for kt in range(KT):
                    last = eng.transpose(psT[:, 0, kt, :], xb[:, p, kt * P:(kt + 1) * P], ident[:])
                c_t1.done(last)

            def project_half(n):
                def project(t, p, h):
                    c_xlo.wait(eng, t)
                    c_res.wait(eng, t - 1, n + 1)
                    c_mm.done(products(psO[:, n, :], p, lambda part, kt: wT[:, part, kt, n * HALF:(n + 1) * HALF]))
                return project

            def transpose_x2(t, p, h):
                c_ln2.wait(eng, t)
                c_queue.wait(eng, t - 3)
                for kt in range(KT):
                    last = eng.transpose(psT[:, 1, kt, :], x2[:, p, kt * P:(kt + 1) * P], ident[:])
                c_t2.done(last)

            def gate(t, p, h):
                c_x2T.wait(eng, t)
                c_top.wait(eng, t - 1, 1)
                for kt in range(KT):
                    last = eng.matmul(psG[:, 0:N_EXP], x2T[:, kt, :], wg[:, kt, :], start=(kt == 0), stop=(kt == KT - 1))
                c_gate.done(last)

            def places(t, p, h):
                c_top.wait(eng, t)
                c_hot.wait(eng, t - 1, 2)
                eng.matmul(psN[:, 0, :], tri[:], chosen[:], start=True, stop=True)
                c_pos.done(eng.matmul(psN[:, 1, :], ones16[:], chosen[:], start=True, stop=True))

            def enqueue(t, p, h):
                c_hot.wait(eng, t)
                c_queue.wait(eng, t - 1)
                for e in range(N_EXP):
                    last = eng.matmul(psQ[:, e * JB:(e + 1) * JB], row_hot[:, e, :], blk_tok[:, e, :], start=True, stop=True)
                c_ids.done(last)

            eng.wait_ge(s_const, NCONST)
            transpose_x(0, 0, 0)
            group_sums(0)
            for r in range(NT):
                if r + 1 < NT:
                    group_sums(r + 1)
                if r == 0:
                    c_xlo.wait(eng, 0)
                if r == NT // 2:
                    c_wlo.wait(eng, r - 1)
                    project_half(0)(0, 0, 0)
                transpose_w(r)
            c_wlo.wait(eng, NT - 1)
            eng.wait_ge(s_small, 48)
            pipeline(eng, [(project_half(0), 0, 1), (transpose_x, 1, 1), (gate, -2), (places, -3), (enqueue, -4),
                           (project_half(1), 0), (transpose_x2, -1)], NB)

            c_tab_d.wait(eng, 0, 1)
            eng.transpose(psT[:, 0, 0, :], queue[:], ident[:])
            c_tab_p.done(eng.matmul(psG[:, 0:1], act_row[:].rearrange("p e j -> p (e j)"), ident[:, 0:1], start=True, stop=True))
            c_tab_d.wait(eng, 0, 3)
            c_tab_p.done(eng.matmul(psG[:, 16:17], tri[:], act_c16[:, 0:1], start=True, stop=True))
            c_tab_d.wait(eng, 0, 8)
            eng.matmul(psG[:, 64:64 + N_BLOCKS], queueT[:], pick[:], start=True, stop=True).then_inc(c_half.sem, NH)
            c_tab_p.done(eng.matmul(psG[:, 128:128 + N_BLOCKS + N_EXP], ones16[:], meta_in[:], start=True, stop=True))

            def transpose_rows(b, p, h):
                l_gather.wait(eng, p, h)
                c_rhi.wait(eng, b - 1)
                for kt in range(KT):
                    last = eng.transpose(psT[:, 0, kt, :], x2[:, p, kt * P:(kt + 1) * P], ident[:])
                c_turn.done(last)

            def expert(b, p, h):
                s = eng.value_load(slot_of[0:1, bass.ds(b, 1)], min_val=0, max_val=1)
                ready = eng.value_load(ready_of[0:1, bass.ds(b, 1)], min_val=2 * KT, max_val=2 * KT * N_EXP)
                c_rlo.wait(eng, b)
                eng.wait_ge(c_split.sem, ready)
                for n in range(NH):
                    cols = slice(n * HALF, (n + 1) * HALF)
                    c_out.wait(eng, b - 1, n + 1)
                    moving = lambda part, kt: slots[:, bass.ds(s, 1), part, kt, cols].rearrange("p a n -> p (a n)")
                    bias = lambda: eng.matmul(psO[:, n, :], ones_bias[:, :],
                                              bias_slot[:, bass.ds(s, 1), cols].rearrange("p a n -> p (a n)"),
                                              start=False, stop=True)
                    c_half.done(products(psO[:, n, :], p, moving, bias))

            c_tab_d.wait(eng, 0, 14)
            c_lo0.wait(eng, NB - 1)
            l_bias.wait(eng, 0, 0)
            pipeline(eng, [(transpose_rows, 1), (expert, 0)], N_BLOCKS)

        @block.scalar
        def _(eng):
            eng.dma_start(bias_raw[:], b_e).then_inc(s_small, 16)
            eng.dma_start(wg[:], w_gate.rearrange("(k p) e -> p k e", p=P)).then_inc(s_small, 16)
            eng.dma_start(bg[:], b_gate.partition_broadcast(P)).then_inc(s_small, 16)

            def x_hi(t, p, h):
                c_t1.wait(eng, t)
                c_mm.wait(eng, t - 2)
                c_xhi.done(eng.activation(xT[:, p, HI, :, :], psT[:, 0, :, :], ACT.Copy))

            def x2_columns(t, p, h):
                c_t2.wait(eng, t)
                c_gate.wait(eng, t - 1)
                c_x2T.done(eng.activation(x2T[:], psT[:, 1, :, :], ACT.Copy))

            def piece_hi(t, p, h):
                l_raw0.wait(eng, p, h)
                c_hi0.done(eng.activation(slots[:, 0, HI, bass.ds(h, 1), p * HALF:(p + 1) * HALF].rearrange("p a n -> p (a n)"),
                                          raw[:, p, 0:HALF], ACT.Copy))

            x_hi(0, 0, 0)
            for r in range(NT):
                c_wt.wait(eng, r)
                c_whi.done(eng.activation(wT[:, HI, :, r * P:(r + 1) * P], psT[:, r % 2, :, :], ACT.Copy))
            eng.wait_ge(s_bstore, 16)
            pipeline(eng, [(x_hi, 1, 1), (piece_hi, 0), (x2_columns, -1)], NB)

            def rows_hi(b, p, h):
                c_turn.wait(eng, b)
                c_half.wait(eng, b - 2)
                c_rhi.done(eng.activation(xT[:, p, HI, :, :], psT[:, 0, :, :], ACT.Copy))
                c_rlo.wait(eng, b - 1)
                c_rhi.done(eng.activation(x2T[:], psT[:, 0, :, :], ACT.Copy))

            def relu_half(b, p, h):
                l_add.wait(eng, p, h - 1)
                for n in range(NH):
                    c_half.wait(eng, b, n + 1)
                    c_out.done(eng.activation(xb[:, p, n * HALF:(n + 1) * HALF], psO[:, n, :], ACT.Relu, scale=1.0 / TOP_K))

            c_mm.wait(eng, NB - 1)
            pipeline(eng, [(rows_hi, 1), (relu_half, 0)], N_BLOCKS)

        @block.vector
        def _(eng):
            eng.wait_ge(s_const, NCONST)
            s_vconst.done(eng.tensor_copy(ones_bias[:], ones16[0:2, :]))
            s_vconst.done(eng.memset(count[:], 0.0))
            s_vconst.done(eng.memset(queue[:], 0.0))
            s_vconst.done(eng.tensor_reduce(eminus[:, 0:1], upto[:], AX.X, ALU.add))
            s_vconst.wait(eng, 3)
            s_vconst.done(eng.tensor_scalar(eminus[:, 1:2], eminus[:, 0:1], -1.0, 1.0, ALU.mult, ALU.add))

            def stats(c, src, which, t, p, landed):
                landed()
                c.wait(eng, t - 1)
                for g in range(2):
                    c.done(eng.bn_stats(st[:, which, g, :], src[:, g * HD:(g + 1) * HD]))
                c.wait(eng, t, 2, alone=s_void)
                c.done(eng.bn_aggr(mv[:, which, p, :], st[:, which, :, :].rearrange("p g s -> p (g s)")))

            def normalise(c, c_which, which, src, dst, t, p):
                c_which.wait(eng, t)
                c.done(eng.tensor_scalar(dst, src, mv[:, which, p, 0:1], rs[:, which, 1:2], ALU.subtract, ALU.mult))

            def norm1(t, p, h):
                normalise(c_ln1, c_rs[0], 0, xb[:, p, :], xb[:, p, :], t, p)

            def norm2(t, p, h):
                l_x2.wait(eng, p, h - 1)
                c_t2.wait(eng, t - 2)
                normalise(c_ln2, c_rs[1], 1, xr[:, p, :], x2[:, p, :], t, p)

            def stats1(t, p, h):
                def landed():
                    l_x.wait(eng, p, h)
                    c_ln1.wait(eng, t - 2)
                stats(c_st1, xb[:, p, :], 0, t, p, landed)

            def stats2(t, p, h):
                def landed():
                    c_res.wait(eng, t)
                    c_ln2.wait(eng, t - 2)
                stats(c_st2, xr[:, p, :], 1, t, p, landed)

            def x_lo(t, p, h):
                c_xhi.wait(eng, t)
                c_xlo.done(eng.tensor_tensor(xT[:, p, LO, :, :], psT[:, 0, :, :], xT[:, p, HI, :, :].bitcast(F32), ALU.subtract))

            def residual(t, p, h):
                l_xr.wait(eng, p, h)
                for n in range(NH):
                    c_mm.wait(eng, t, n + 1)
                    cols = slice(n * HALF, (n + 1) * HALF)
                    c_res.done(eng.tensor_tensor(xr[:, p, cols], xr[:, p, cols], psO[:, n, :], ALU.add))

            def top2(t, p, h):
                c_gate.wait(eng, t)
                c_pos.wait(eng, t - 1)
                c_hot.wait(eng, t - 2)
                c_top.wait(eng, t - 1)
                mine = logit[:].unsqueeze(2).to_broadcast([P, N_EXP, N_EXP])
                other = logit[:].unsqueeze(1).to_broadcast([P, N_EXP, N_EXP])
                c_top.done(eng.tensor_tensor(logit[:], psG[:, 0:N_EXP], bg[:], ALU.add))
                c_top.wait(eng, t, 1)
                c_top.done(eng.tensor_tensor(eq[:], other, mine, ALU.is_equal))
                c_top.done(eng.tensor_tensor(gt[:], other, mine, ALU.is_gt))
                c_top.wait(eng, t, 2)
                c_top.done(eng.tensor_tensor(eq[:], eq[:], tri_e[:], ALU.mult))
                c_top.wait(eng, t, 4)
                c_top.done(eng.tensor_tensor(gt[:], gt[:], eq[:], ALU.add))
                c_top.wait(eng, t, 5)
                c_top.done(eng.tensor_reduce(rank[:], gt[:], AX.X, ALU.add))
                c_top.wait(eng, t, 6)
                c_top.done(eng.tensor_scalar(chosen_tok[:, p, :], rank[:], float(TOP_K), tok[:, 0:1], ALU.is_lt, ALU.mult))
                c_top.done(eng.tensor_scalar(chosen[:], rank[:], float(TOP_K), None, ALU.is_lt))
                c_top.wait(eng, t, 7)
                c_top.done(eng.tensor_scalar(tok[:], tok[:], float(P), None, ALU.add))

            def one_hots(t, p, h):
                c_pos.wait(eng, t)
                c_hot.wait(eng, t - 1)
                c_hot.done(eng.tensor_tensor(pos[:], psN[:, 0, :], count[:], ALU.add))
                c_hot.wait(eng, t, 1)
                c_hot.done(eng.tensor_tensor(count[:], count[:], psN[:, 1, :], ALU.add))
                c_hot.done(eng.tensor_copy(pos_i[:], pos[:]))
                c_hot.wait(eng, t, 3)
                c_hot.done(eng.tensor_scalar(pos_r[:], pos_i[:], P - 1, None, ALU.bitwise_and))
                c_hot.done(eng.tensor_scalar(pos_j[:], pos_i[:], P.bit_length() - 1, None, ALU.logical_shift_right))
                c_hot.wait(eng, t, 5)
                c_ids.wait(eng, t - 1)
                c_hot.done(eng.tensor_tensor(blk_hot[:], lane[:, 0:JB].unsqueeze(1).to_broadcast([P, N_EXP, JB]),
                                             pos_j[:].unsqueeze(2).to_broadcast([P, N_EXP, JB]), ALU.is_equal))
                c_hot.done(eng.tensor_tensor(row_hot[:], lane[:].unsqueeze(1).to_broadcast([P, N_EXP, P]),
                                             pos_r[:].unsqueeze(2).to_broadcast([P, N_EXP, P]), ALU.is_equal))
                c_hot.wait(eng, t, 6)
                c_hot.done(eng.tensor_tensor(blk_tok[:], blk_hot[:],
                                             chosen_tok[:, p, :].unsqueeze(2).to_broadcast([P, N_EXP, JB]), ALU.mult))

            def add_queue(t, p, h):
                c_ids.wait(eng, t)
                c_queue.wait(eng, t - 1)
                c_queue.done(eng.tensor_tensor(queue[:], queue[:], psQ, ALU.add))

            def split_chunk(e_slot, kt, q):
                l_raw.wait(eng, kt % 2, q)
                c = KT + 2 * q + kt % 2
                c_split.done(eng.tensor_copy(slots[:, e_slot, HI, kt, :], raw[:, kt % 2, :]))
                c_split.wait(eng, c, 1)
                c_split.done(eng.tensor_tensor(slots[:, e_slot, LO, kt, :], raw[:, kt % 2, :],
                                               slots[:, e_slot, HI, kt, :].bitcast(F32), ALU.subtract))

            def split_expert(e_slot, e_half, q0):
                for kt in range(KT):
                    if kt == KT - 1:
                        l_bias.wait(eng, e_slot, e_half)
                    split_chunk(e_slot, kt, q0 + kt // 2)

            for t in range(2):
                stats1(t, t, 0)
                norm1(t, t, 0)
            x_lo(0, 0, 0)
            def w_lo(r):
                c_whi.wait(eng, r)
                here = slice(r * P, (r + 1) * P)
                c_wlo.done(eng.tensor_tensor(wT[:, LO, :, here], psT[:, r % 2, :, :], wT[:, HI, :, here].bitcast(F32), ALU.subtract))

            for r in range(NT):
                eng.wait_ge(s_m[r], 16)
                c_msum.done(eng.tensor_reduce(msum[:, r, :], mask_stage[:, r, :].rearrange("p (g s) -> p g s", s=SUB),
                                              AX.X, ALU.add))
                c_group.wait(eng, r)
                c_em.done(eng.tensor_scalar(emask[:, r, :], psG[:, 0:NSUB], 0.0, None, ALU.is_gt))
                if r > 1:
                    w_lo(r - 2)
            eng.wait_ge(s_small, 48)
            c_bsplit.done(eng.tensor_copy(bias_hl[:, HI, :], bias_raw[:]))
            c_bsplit.wait(eng, 0)
            c_bsplit.done(eng.tensor_tensor(bias_hl[:, LO, :], bias_raw[:], bias_hl[:, HI, :].bitcast(F32), ALU.subtract))
            w_lo(NT - 2)
            w_lo(NT - 1)
            eng.wait_ge(s_bstore, 16)
            pipeline(eng, [(residual, -1), (stats2, -1), (stats1, 2, 2), (norm2, -1), (norm1, 2, 2), (x_lo, 1, 1),
                           (top2, -2), (one_hots, -3), (add_queue, -4)], NB)

            c_hot.wait(eng, NB - 1)
            c_queue.wait(eng, NB - 1)
            for p in range(2):
                l_x1.wait(eng, p, NB // 2 - 1)
            c_ln2.wait(eng, NB - 1)
            tab = c_tab_d
            tab.done(eng.tensor_tensor(act_row[:], count[:].unsqueeze(2).to_broadcast([P, N_EXP, JB]),
                                       lane_first[:].unsqueeze(1).to_broadcast([P, N_EXP, JB]), ALU.is_gt))
            c_tab_p.wait(eng, 0, 1)
            tab.done(eng.tensor_copy(act_col[:, 0:1], psG[:, 0:1]))
            tab.done(eng.tensor_copy(act_c16[:, 0:1], psG[:, 0:1]))
            tab.done(eng.tensor_copy(queueT[:], psT[:, 0, 0, :]))
            c_tab_p.wait(eng, 0, 2)
            tab.done(eng.tensor_copy(act_col[:, 1:2], psG[:, 16:17]))
            tab.wait(eng, 0, 5)
            tab.done(eng.tensor_scalar(pick[:], lane[:, 0:N_BLOCKS], act_col[:, 1:2], act_col[:, 0:1], ALU.is_equal, ALU.mult))
            tab.done(eng.tensor_scalar(meta_in[:, N_BLOCKS:], upto[:], act_col[:, 0:1], None, ALU.mult))
            tab.wait(eng, 0, 6)
            tab.done(eng.tensor_scalar(meta_in[:, 0:N_BLOCKS], pick[:], eminus[:, 1:2], None, ALU.mult))
            c_tab_p.wait(eng, 0, 3)
            tab.done(eng.tensor_scalar(empty[:], psG[:, 64:64 + N_BLOCKS], 0.0, spare[:, 0:1], ALU.is_equal, ALU.mult))
            tab.done(eng.tensor_scalar(e_of[:], psG[:, 128:128 + N_BLOCKS], float(N_EXP - 1), None, ALU.add))
            tab.done(eng.tensor_scalar(through[:], psG[:, 128 + N_BLOCKS:128 + N_BLOCKS + N_EXP], float(NH), float(NH), ALU.mult, ALU.add))
            tab.wait(eng, 0, 10)
            tab.done(eng.scalar_tensor_tensor(tok_of[:], psG[:, 64:64 + N_BLOCKS], -1.0, empty[:], ALU.add, ALU.add))
            tab.done(eng.tensor_scalar(slot_of[:], e_of[:], 1, None, ALU.bitwise_and))
            tab.done(eng.tensor_scalar(ready_of[:], e_of[:], 1.0, float(2 * KT), ALU.add, ALU.mult))

            c_mm.wait(eng, NB - 1)
            split_expert(1, 0, 0)
            tab.wait(eng, 0, 14)
            with eng.Fori(1, N_EXP // 2) as g:
                for s in range(2):
                    used = eng.value_load(through[0:1, bass.ds(2 * g + s - 2, 1)], min_val=NH, max_val=NH * (N_BLOCKS + 1))
                    eng.wait_ge(c_half.sem, used)
                    split_expert(s, g, KT * g + (s - 1) * KT // 2)

        @block.gpsimd
        def _(eng):
            def const(instruction):
                instruction.then_inc(s_const, 1)

            const(eng.memset(ident[:], 0.0))
            const(eng.memset(group[:], 1.0))
            const(eng.memset(tri[:], 1.0))
            const(eng.memset(ones16[:], 1.0))
            const(eng.memset(tri_e[:], 1.0))
            const(eng.memset(upto[:], 1.0))
            const(eng.memset(raw[:, 0, :], 0.0))
            const(eng.memset(half_neg[:], -0.5))
            eng.memset(rs[:], 0.0).then_inc(c_split.sem, 2 * KT)
            const(eng.iota(lane[:], [[1, P]], base=0, channel_multiplier=0, allow_small_or_imprecise_dtypes=True))
            const(eng.iota(lane_first[:], [[P, JB]], base=0, channel_multiplier=0, allow_small_or_imprecise_dtypes=True))
            const(eng.iota(tok[:], [[0, 1]], base=1, channel_multiplier=1, allow_small_or_imprecise_dtypes=True))
            eng.wait_ge(s_const, 11)
            const(eng.iota(spare[:], [[0, 1]], base=N_TOK + 1, channel_multiplier=1, allow_small_or_imprecise_dtypes=True))
            const(eng.affine_select(out=ident[:], in_=ident[:], pattern=[[-1, P]], compare_op=ALU.not_equal, fill=1.0,
                                    base=0, channel_multiplier=1))
            g4 = group[:].rearrange("p (g s) -> p g s", s=SUB)
            const(eng.affine_select(out=g4, in_=g4, pattern=[[-SUB, P // SUB], [0, SUB]], compare_op=ALU.is_ge, fill=0.0,
                                    base=0, channel_multiplier=1))
            const(eng.affine_select(out=tri[:], in_=tri[:], pattern=[[1, P]], compare_op=ALU.is_ge, fill=0.0,
                                    base=-1, channel_multiplier=-1))
            const(eng.affine_select(out=tri_e[:], in_=tri_e[:], pattern=[[1, N_EXP], [-1, N_EXP]], compare_op=ALU.is_ge,
                                    fill=0.0, base=-1, channel_multiplier=0))
            const(eng.affine_select(out=upto[:], in_=upto[:], pattern=[[JB, N_EXP]], compare_op=ALU.is_ge, fill=0.0,
                                    base=JB - 1, channel_multiplier=-1))
            eng.wait_ge(s_const, 17)
            const(eng.affine_select(out=g4, in_=g4, pattern=[[SUB, P // SUB], [0, SUB]], compare_op=ALU.is_ge, fill=0.0,
                                    base=SUB - 1, channel_multiplier=-1))

            def inverse_std(which, stats_done):
                c = c_rs[which]

                def run(t, p, h):
                    c.wait(eng, t - 1)
                    (c_ln1, c_ln2)[which].wait(eng, t - 1)
                    stats_done.wait(eng, t, alone=s_void)
                    c.done(eng.tensor_scalar(rs[:, which, 0:1], mv[:, which, p, 1:2], EPS, None, ALU.add))
                    c.wait(eng, t, 1)
                    c.done(eng.tensor_tensor(rs[:, which, 1:2], rs[:, which, 0:1], half_neg[:], ALU.pow))
                return run

            def piece_lo(t, p, h):
                c_hi0.wait(eng, t)
                cols = slice(p * HALF, (p + 1) * HALF)
                c_lo0.done(eng.tensor_tensor(slots[:, 0, LO, bass.ds(h, 1), cols].rearrange("p a n -> p (a n)"), raw[:, p, 0:HALF],
                                             slots[:, 0, HI, bass.ds(h, 1), cols].rearrange("p a n -> p (a n)").bitcast(F32), ALU.subtract))

            inverse_std(0, c_st1)(0, 0, 0)
            inverse_std(0, c_st1)(1, 1, 0)
            for r in range(NT):
                c_em.wait(eng, r)
                eng.wait_ge(s_w[r], 16)
                rows = w_stage[:, r, :].rearrange("p (g s) -> p g s", s=SUB)
                c_wm.done(eng.tensor_tensor(rows, rows, emask[:, r, :].unsqueeze(2).to_broadcast([P, NSUB, SUB]), ALU.mult))
            c_wt.wait(eng, NT - 1)
            pipeline(eng, [(inverse_std(1, c_st2), -1), (inverse_std(0, c_st1), 2, 2), (piece_lo, 0)], NB)

            def set_tokens(which, b, p):
                c_tok[which].done(eng.tensor_copy(tok_at[:, which, p:p + 1], tok_of[:, bass.ds(b, 1)]))
                c_tok[which].wait(eng, b, alone=s_void)

            def by_token(which, p):
                return bass.IndirectOffsetOnAxis(ap=tok_at[:, which, p:p + 1], axis=0)

            def gather_rows(b, p, h):
                c_turn.wait(eng, b - 2)
                set_tokens(GATHER, b, p)
                l_gather.done(eng.indirect_dma_start(x2[:, p, :], None, x2_rows, by_token(GATHER, p),
                                                     bounds_check=N_TOK - 1, oob_is_err=False), p)

            def rows_lo(b, p, h):
                c_rhi.wait(eng, b)
                c_rlo.done(eng.tensor_tensor(xT[:, p, LO, :, :], x2T[:], xT[:, p, HI, :, :].bitcast(F32), ALU.subtract))

            def add_rows(b, p, h):
                if isinstance(b, int):
                    if b > 0:
                        l_add.wait(eng, 1 - p, (b - 1) // 2)
                else:
                    l_add.wait(eng, 1 - p, h if p == 1 else h - 1)
                set_tokens(ADD, b, p)
                c_out.wait(eng, b, alone=s_void)
                l_add.done(eng.indirect_dma_start(out, by_token(ADD, p), xb[:, p, :], None, bounds_check=N_TOK + P - 1,
                                                  compute_op=ALU.add), p)

            for p in range(2):
                l_x1.wait(eng, p, NB // 2 - 1)
                l_x2.wait(eng, p, NB // 2 - 1)
            eng.wait_ge(s_spare, 16)
            c_tab_d.wait(eng, 0, 12)
            pipeline(eng, [(gather_rows, 2), (rows_lo, 1), (add_rows, 0)], N_BLOCKS)
            for p in range(2):
                l_add.wait(eng, p, (N_BLOCKS - 1 - p) // 2)


_INS = ["L0_attn_data", "L0_attn_weight", "L0_attn_mask", "L0_ffn_W_gate", "L0_ffn_b_gate", "L0_ffn_W_e", "L0_ffn_b_e"]


def kernel(**inputs):
    import numpy as np
    import concourse.bacc as bacc
    from concourse.bass_utils import run_bass_kernel_spmd

    nc = bacc.Bacc("TRN2", target_bir_lowering=False, num_devices=1)
    B, S, D = inputs["L0_attn_data"].shape
    arrays, args = {}, []
    for name in _INS:
        a = np.ascontiguousarray(inputs[name])
        if name == "L0_attn_data":
            a = a.reshape(B * S, D)
        arrays[name] = a
        args.append(nc.dram_tensor(name, a.shape, mybir.dt.from_np(a.dtype), kind="ExternalInput").ap())
    args.append(nc.dram_tensor("rows_out", (B * S + P, D), F32, kind="ExternalOutput").ap())
    build(nc, *args)
    r = run_bass_kernel_spmd(nc, [arrays], core_ids=[0])
    return r.results[0]["rows_out"][:B * S].reshape(B, S, D)
```

```python
from contextlib import ExitStack

import concourse.bass as bass
from concourse import mybir

F32 = mybir.dt.float32
F32R = mybir.dt.float32r
F16 = mybir.dt.float16
I32 = mybir.dt.int32
ALU = mybir.AluOpType
ACT = mybir.ActivationFunctionType
AX = mybir.AxisListType

P = 128
EPS = 1e-5
TOP_K = 2
HI, LO = 0, 1
GATHER, ADD = 0, 1
PASSES = [(HI, HI), (HI, LO), (LO, HI)]


class Chain:

    def __init__(self, sem, steps=1, base=0):
        self.sem, self.steps, self.base = sem, steps, base

    def done(self, instruction):
        instruction.then_inc(self.sem, 1)

    def wait(self, engine, block, step=None, alone=None):
        value = self.base + block * self.steps + (self.steps if step is None else step)
        if not isinstance(value, int) or value > 0:
            engine.wait_ge(self.sem, value)
            if alone is not None and not isinstance(value, int):
                engine.sem_inc(alone, 1)


class Landings:

    def __init__(self, sems):
        self.sems = sems

    def done(self, instruction, parity):
        instruction.then_inc(self.sems[parity], 16)

    def wait(self, engine, parity, half):
        value = 16 * half + 16
        if not isinstance(value, int) or value > 0:
            engine.wait_ge(self.sems[parity], value)


def pipeline(engine, stages, n):
    stages = [(s[0], s[1], s[2] if len(s) > 2 else 0, s[3] if len(s) > 3 else n) for s in stages]
    leads = [s[1] for s in stages]
    first, last = -max(leads), n - min(leads)
    start = -min(leads) + 2
    turns = (n - max(leads) - start) // 2

    def peeled(lo, hi):
        for i in range(lo, hi):
            for stage, lead, from_block, end in stages:
                b = i + lead
                if from_block <= b < end:
                    stage(b, b % 2, b // 2)

    if turns < 2:
        peeled(first, last)
        return
    peeled(first, start)
    with engine.Fori(0, turns) as j:
        for u in range(2):
            for stage, lead, _, _ in stages:
                base = start + u + lead
                stage(2 * j + base, base % 2, j + base // 2)
    peeled(start + 2 * turns, last)


def build(nc, data, weight, mask, w_gate, b_gate, w_e, b_e, out):
    N_TOK, D = data.shape
    N_EXP, _, H = w_e.shape
    KT = D // P
    NB = N_TOK // P
    HALF = 512
    NH = H // HALF
    NT = D // P
    SUB = 32
    NSUB = D // SUB
    JB = N_TOK // P
    NC = N_EXP * JB
    N_BLOCKS = (TOP_K * N_TOK + N_EXP * (P - 1)) // P
    assert D == 1024 and H == D and weight.shape == (D, D) and NC == P and N_EXP == 8
    HD = D // 2

    ctx = ExitStack()
    with ctx:
        x2_rows = nc.dram_tensor("x2_rows", (N_TOK, D), F32, kind="Internal").ap()

        cursor = [(nc.sbuf_base + 63) // 64 * 64]

        def at(name, shape, dt, offset):
            return nc.alloc_sbuf_tensor_at(name, shape, dt, offset=offset)

        def sb(name, shape, dt):
            size = 1
            for s in shape[1:]:
                size *= s
            size *= 2 if dt == F16 else 4
            t = at(name, shape, dt, cursor[0])
            cursor[0] += (size + 31) // 32 * 32
            return t

        slot_base = cursor[0]
        slots = sb("slots", [P, 2, 2, KT, H], F32R)
        slot_bytes = 2 * KT * H * 4
        w_stage = at("w_stage", [P, NT, D], F32, slot_base)
        mask_stage = at("mask_stage", [P, NT, D], I32, slot_base + NT * D * 4)
        wT = at("wT", [P, 2, KT, D], F32R, slot_base + slot_bytes)

        raw = sb("raw", [P, 2, H], F32)
        bias_slot = sb("bias_slot", [P, 2, H], F32)
        xb = sb("xb", [P, 2, D], F32)
        xr_offset = cursor[0]
        xr = sb("xr", [P, 2, D], F32)
        xT = sb("xT", [P, 2, 2, KT, P], F32R)
        x2 = sb("x2", [P, 2, D], F32)
        x2T = sb("x2T", [P, KT, P], F32)

        ident = sb("ident", [P, P], F32)
        group = sb("group", [P, P], F32)
        msum = sb("msum", [P, NT, NSUB], F32)
        emask = sb("emask", [P, NT, NSUB], F32)
        tri = sb("tri", [P, P], F16)
        ones16 = sb("ones16", [P, P], F16)
        lane = sb("lane", [P, P], F16)
        lane_first = sb("lane_first", [P, JB], F32)
        tri_e = sb("tri_e", [P, N_EXP, N_EXP], F32)
        upto = sb("upto", [P, N_EXP], F32)
        eminus = sb("eminus", [P, 2], F32)
        tok = sb("tok", [P, 1], F32)
        spare = sb("spare", [P, 1], F32)
        half_neg = sb("half_neg", [P, 1], F32)
        wg = sb("wg", [P, KT, N_EXP], F32)
        wg_part = sb("wg_part", [P, N_EXP], F32)
        wg_sum = sb("wg_sum", [P, N_EXP], F32)
        gates = sb("gates", [P, KT, 2, 2, N_EXP], F32R)
        fold = sb("fold", [4 * N_EXP, 2 * N_EXP], F32)
        gated = sb("gated", [4 * N_EXP, P], F32)
        ones = sb("ones", [P, P], F32)
        foldedT = sb("foldedT", [N_EXP, NH, HALF], F32)
        kept = sb("kept", [P, NB, 2], F32)
        bg = sb("bg", [P, N_EXP], F32)
        st = sb("st", [P, 2, 2, 6], F32)
        mv = sb("mv", [P, 2, 2, 2], F32)
        rs = sb("rs", [P, 2, 4], F32)
        share = sb("share", [P, N_EXP], F32)
        logit = sb("logit", [P, N_EXP], F32)
        gt = sb("gt", [P, N_EXP, N_EXP], F32)
        eq = sb("eq", [P, N_EXP, N_EXP], F32)
        rank = sb("rank", [P, N_EXP], F32)
        chosen = sb("chosen", [P, N_EXP], F16)
        chosen_tok = sb("chosen_tok", [P, 2, N_EXP], F32)
        count = sb("count", [P, N_EXP], F32)
        pos = sb("pos", [P, N_EXP], F32)
        pos_i = sb("pos_i", [P, N_EXP], I32)
        pos_r = sb("pos_r", [P, N_EXP], I32)
        pos_j = sb("pos_j", [P, N_EXP], I32)
        row_hot = sb("row_hot", [P, N_EXP, P], F16)
        blk_hot = sb("blk_hot", [P, N_EXP, JB], F16)
        blk_tok = sb("blk_tok", [P, N_EXP, JB], F16)
        queue = sb("queue", [P, NC], F32)
        end, cursor[0] = cursor[0], xr_offset
        act_row = sb("act_row", [P, N_EXP, JB], F32)
        act_col = sb("act_col", [P, 2], F32)
        act_c16 = sb("act_c16", [P, 2], F16)
        queueT = sb("queueT", [P, P], F32)
        pick = sb("pick", [P, N_BLOCKS], F32)
        meta_in = sb("meta_in", [P, N_BLOCKS + N_EXP], F16)
        empty = sb("empty", [P, N_BLOCKS], F32)
        tok_of = sb("tok_of", [P, N_BLOCKS], I32)
        tok_at = sb("tok_at", [P, 2, 2], I32)
        e_of = sb("e_of", [P, N_BLOCKS], I32)
        slot_of = sb("slot_of", [P, N_BLOCKS], I32)
        ready_of = sb("ready_of", [P, N_BLOCKS], I32)
        through = sb("through", [P, N_EXP], I32)
        assert cursor[0] <= xr_offset + 2 * D * 4 and end <= nc.sbuf_usable_end

        def ps(name, shape, dt=F32):
            return ctx.enter_context(nc.psum_tensor(name, shape, dt))

        psT = ps("psT", [P, 2, KT, P])
        psO = ps("psO", [P, NH, HALF])
        psG = ps("psG", [P, HALF])
        psS = ps("psS", [P, HALF])
        psN = psS[:, 0:2 * N_EXP].rearrange("p (a e) -> p a e", e=N_EXP)
        psF = [psO[0:N_EXP, 1, :], psS[0:N_EXP, :]]
        psU = psG[:, 64:64 + KT * N_EXP]
        psW = psG[:, 256:256 + N_EXP]
        psL = psT[:, 1, KT // 2, 0:2 * N_EXP]
        psQ = psT[:, 1, 0, :]

        def sem(name):
            return ctx.enter_context(nc.semaphore(name))

        def chain(name, steps=1):
            return Chain(sem(name), steps)

        def landings(name):
            return Landings([sem(name + "_even"), sem(name + "_odd")])

        s_void = sem("s_void")
        s_const, s_vconst, s_small = sem("s_const"), chain("s_vconst"), sem("s_small")
        s_w = [sem(f"s_w{r}") for r in range(NT)]
        s_m = [sem(f"s_m{r}") for r in range(NT)]
        l_x, l_xr, l_raw, l_raw0, l_bias = (landings(n) for n in ("l_x", "l_xr", "l_raw", "l_raw0", "l_bias"))
        l_x1, l_x2 = landings("l_x1"), landings("l_x2")
        l_gather, l_add = landings("l_gather"), landings("l_add")
        s_spare = sem("s_spare")
        c_msum, c_em, c_wm, c_wlo = chain("c_msum"), chain("c_em"), chain("c_wm"), chain("c_wlo")
        c_group, c_wt, c_whi = chain("c_group"), chain("c_wt"), chain("c_whi")
        c_st1, c_ln1, c_t1, c_xhi, c_xlo = chain("c_st1", 3), chain("c_ln1"), chain("c_t1"), chain("c_xhi"), chain("c_xlo")
        c_mm, c_res, c_st2, c_ln2 = chain("c_mm", NH), chain("c_res", NH), chain("c_st2", 3), chain("c_ln2")
        c_rs = [chain("c_rs1", 5), chain("c_rs2", 4)]
        c_prep, c_part, c_fold, c_gw = chain("c_prep"), chain("c_part"), chain("c_fold"), chain("c_gw", 5)
        c_fold_read, c_unfold = chain("c_fold_read"), chain("c_unfold")
        c_gate, c_gated, c_logit = chain("c_gate"), chain("c_gated"), chain("c_logit")
        c_top, c_pos, c_hot, c_ids, c_queue = chain("c_top", 12), chain("c_pos"), chain("c_hot", 8), chain("c_ids"), chain("c_queue")
        c_tab_d, c_tab_p = chain("c_tab_d"), chain("c_tab_p")
        c_hi0, c_lo0, c_split = chain("c_hi0"), chain("c_lo0"), chain("c_split", 2)
        c_turn, c_rhi, c_rlo, c_half = chain("c_turn"), chain("c_rhi", 2), chain("c_rlo"), Chain(sem("c_half"), NH, NH)
        c_tok = [chain("c_tok_gather"), chain("c_tok_add")]
        c_out, c_seed = chain("c_out", NH), chain("c_seed", NH)

        def w_half_of(r):
            return 1 if r == 0 else r % 2

        block = ctx.enter_context(nc.Block())
        NCONST = 19
        PASS_AT = NT // 2
        X1_AT = NT - 2

        @block.sync
        def _(eng):
            def load_x(t, p, h):
                c_t1.wait(eng, t - 2)
                l_x.done(eng.dma_start(xb[:, p, :], data[bass.ds(t * P, P), :]), p)

            def load_residual(t, p, h):
                l_x1.wait(eng, p, h - 1)
                c_ln2.wait(eng, t - 2, alone=s_void)
                l_xr.done(eng.dma_start(xr[:, p, :], data[bass.ds(t * P, P), :]), p)

            def store_x1(t, p, h):
                c_res.wait(eng, t)
                l_x1.done(eng.dma_start(out[bass.ds(t * P, P), :], xr[:, p, :]), p)

            def store_x2(t, p, h):
                c_ln2.wait(eng, t)
                l_x2.done(eng.dma_start(x2_rows[bass.ds(t * P, P), :], x2[:, p, :]), p)

            def load_piece(t, p, h):
                c_lo0.wait(eng, t - 2, alone=s_void)
                l_raw0.done(eng.dma_start(raw[:, p, 0:HALF], w_e[0, bass.ds(h * P, P), p * HALF:(p + 1) * HALF]), p)

            def load_chunk(e, kt, q):
                c_split.wait(eng, KT + 2 * q + kt % 2 - 2)
                l_raw.done(eng.dma_start(raw[:, kt % 2, :], w_e[bass.ds(e, 1), kt * P:(kt + 1) * P, :]
                                         .rearrange("e p h -> p (e h)")), kt % 2)

            def load_bias(e, s):
                l_bias.done(eng.dma_start(bias_slot[:, s, :], b_e[bass.ds(e, 1), :].rearrange("e h -> (e h)")
                                          .partition_broadcast(P)), s)

            for r in range(NT):
                rows = slice(r * P, (r + 1) * P)
                if r == 1:
                    load_x(0, 0, 0)
                if r == X1_AT - 1:
                    load_x(1, 1, 0)
                eng.dma_start(mask_stage[:, r, :], mask[rows, :]).then_inc(s_m[r], 16)
                eng.dma_start(w_stage[:, r, :], weight[rows, :]).then_inc(s_w[r], 16)
            eng.wait_ge(s_const, NCONST)
            eng.dma_start(out[N_TOK:N_TOK + P, :], raw[:, 0, :]).then_inc(s_spare, 16)
            eng.wait_ge(s_spare, 16)
            pipeline(eng, [(load_residual, 0), (store_x1, -1), (load_piece, 0), (load_x, 3, 2), (store_x2, -1)], NB)
            load_bias(0, 0)
            for p in range(2):
                c_lo0.wait(eng, NB - 2 + p)
            for kt in range(KT):
                load_chunk(1, kt, kt // 2)
            load_bias(1, 1)
            with eng.Fori(1, N_EXP // 2) as g:
                for s in range(2):
                    for kt in range(KT):
                        load_chunk(2 * g + s, kt, KT * g + (s - 1) * KT // 2 + kt // 2)
                    load_bias(2 * g + s, s)

        @block.tensor
        def _(eng):
            def one_pass(i, psum, p, moving, seeded=False):
                a, b = PASSES[i]
                for kt in range(KT):
                    last = eng.matmul(psum, xT[:, p, a, kt, :], moving(b, kt), start=(i == 0 and kt == 0 and not seeded),
                                      stop=(i == len(PASSES) - 1 and kt == KT - 1), skip_group_check=seeded)
                return last

            def products(*args):
                for i in range(len(PASSES)):
                    last = one_pass(i, *args)
                return last

            def group_sums(r):
                c_msum.wait(eng, r)
                c_em.wait(eng, r - 1)
                c_group.done(eng.matmul(psG[:, 0:NSUB], group[:], msum[:, r, :], start=True, stop=True))

            def transpose_w(r):
                c_wm.wait(eng, r)
                if r == 2:
                    c_xlo.wait(eng, 0)
                else:
                    before = 0 if r == 1 else r - 2
                    c_whi.wait(eng, before)
                    c_wlo.wait(eng, before)
                for kt in range(KT):
                    last = eng.transpose(psT[:, w_half_of(r), kt, :], w_stage[:, r, kt * P:(kt + 1) * P], ident[:])
                c_wt.done(last)

            def transpose_x(t, p, h):
                c_ln1.wait(eng, t)
                c_xlo.wait(eng, t - 1)
                for kt in range(KT):
                    last = eng.transpose(psT[:, 0, kt, :], xb[:, p, kt * P:(kt + 1) * P], ident[:])
                c_t1.done(last)

            def w_half(n):
                return lambda part, kt: wT[:, part, kt, n * HALF:(n + 1) * HALF]

            def project_half(n):
                def project(t, p, h):
                    c_xlo.wait(eng, t)
                    c_res.wait(eng, t - 1, n + 1)
                    c_mm.done(products(psO[:, n, :], p, w_half(n)))
                return project

            def gate(t, p, h):
                c_gw.wait(eng, 0)
                c_gated.wait(eng, t - 1)
                for part in (HI, LO):
                    for kt in range(KT):
                        last = eng.matmul(psG[0:4 * N_EXP, 0:P], gates[:, kt, :, :, :].rearrange("p a b e -> p (a b e)"),
                                          xT[:, p, part, kt, :], start=(part == HI and kt == 0),
                                          stop=(part == LO and kt == KT - 1))
                c_gate.done(last)

            def gate_columns(t, p, h):
                c_gated.wait(eng, t)
                c_top.wait(eng, t - 1, 2)
                c_logit.done(eng.matmul(psL, gated[:], fold[:], start=True, stop=True))

            def places(t, p, h):
                c_top.wait(eng, t, 10)
                c_hot.wait(eng, t - 1, 2)
                eng.matmul(psN[:, 0, :], tri[:], chosen[:], start=True, stop=True)
                c_pos.done(eng.matmul(psN[:, 1, :], ones16[:], chosen[:], start=True, stop=True))

            def enqueue(t, p, h):
                c_hot.wait(eng, t)
                c_queue.wait(eng, t - 1)
                for e in range(N_EXP):
                    last = eng.matmul(psQ[:, e * JB:(e + 1) * JB], row_hot[:, e, :], blk_tok[:, e, :], start=True, stop=True)
                c_ids.done(last)

            def fold_gate(r):
                c_wm.wait(eng, r)
                for n in range(NH):
                    last = eng.matmul(psF[n], wg[:, r, :], w_stage[:, r, n * HALF:(n + 1) * HALF],
                                      start=(r == 0), stop=(r == NT - 1))
                if r == NT - 1:
                    c_fold.done(last)

            eng.wait_ge(s_const, NCONST)
            group_sums(0)
            group_sums(1)
            for r in range(NT):
                transpose_w(r)
                if r == 0:
                    transpose_x(0, 0, 0)
                if r == 0:
                    eng.wait_ge(s_small, 32)
                fold_gate(r)
                if r + 2 < NT:
                    group_sums(r + 2)
                i = r - PASS_AT
                if i == 0:
                    c_wlo.wait(eng, NT // 2 - 1)
                    c_xlo.wait(eng, 0)
                if 0 <= i < len(PASSES):
                    last = one_pass(i, psO[:, 0, :], 0, w_half(0))
                    if i == len(PASSES) - 1:
                        c_mm.done(last)
            c_part.wait(eng, 0)
            c_em.wait(eng, NT - 1)
            eng.matmul(psW, ones[:], wg_part[:], start=True, stop=True)
            c_wlo.wait(eng, NT - 2)
            transpose_x(1, 1, 0)
            c_fold_read.wait(eng, 0)
            for kt in range(KT):
                last = eng.transpose(psU[:, kt * N_EXP:(kt + 1) * N_EXP],
                                     foldedT[:, kt // (KT // NH), kt % (KT // NH) * P:(kt % (KT // NH) + 1) * P],
                                     ident[0:N_EXP, 0:N_EXP])
            c_unfold.done(last)
            c_wlo.wait(eng, NT - 1)
            project_half(1)(0, 0, 0)
            pipeline(eng, [(gate_columns, -1), (project_half(0), 0, 1), (transpose_x, 1, 2), (enqueue, -2),
                           (gate, 0), (places, -1), (project_half(1), 0, 1)], NB)

            c_tab_d.wait(eng, 0, 1)
            c_tab_p.done(eng.matmul(psG[:, 0:1], act_row[:].rearrange("p e j -> p (e j)"), ident[:, 0:1], start=True, stop=True))
            c_queue.wait(eng, NB - 1)
            c_tab_p.done(eng.transpose(psT[:, 0, 0, :], queue[:], ident[:]))
            c_tab_d.wait(eng, 0, 3)
            c_tab_p.done(eng.matmul(psG[:, 16:17], tri[:], act_c16[:, 0:1], start=True, stop=True))
            c_tab_d.wait(eng, 0, 8)
            eng.matmul(psG[:, 64:64 + N_BLOCKS], queueT[:], pick[:], start=True, stop=True).then_inc(c_half.sem, NH)
            c_tab_p.done(eng.matmul(psG[:, 128:128 + N_BLOCKS + N_EXP], ones16[:], meta_in[:], start=True, stop=True))

            def transpose_rows(b, p, h):
                l_gather.wait(eng, p, h)
                c_rhi.wait(eng, b - 2)
                if isinstance(b, int) and b == 2:
                    c_rlo.wait(eng, 0)
                for kt in range(KT):
                    last = eng.transpose(psT[:, p, kt, :], x2[:, p, kt * P:(kt + 1) * P], ident[:])
                c_turn.done(last)

            def expert(b, p, h):
                s = eng.value_load(slot_of[0:1, bass.ds(b, 1)], min_val=0, max_val=1)
                ready = eng.value_load(ready_of[0:1, bass.ds(b, 1)], min_val=2 * KT, max_val=2 * KT * N_EXP)
                c_rlo.wait(eng, b)
                eng.wait_ge(c_split.sem, ready)
                for n in range(NH):
                    cols = slice(n * HALF, (n + 1) * HALF)
                    c_seed.wait(eng, b, n + 1)
                    moving = lambda part, kt: slots[:, bass.ds(s, 1), part, kt, cols].rearrange("p a n -> p (a n)")
                    c_half.done(products(psO[:, n, :], p, moving, True))

            c_tab_d.wait(eng, 0, 14)
            c_lo0.wait(eng, NB - 1)
            pipeline(eng, [(transpose_rows, 1), (expert, 0)], N_BLOCKS)

        @block.scalar
        def _(eng):
            eng.dma_start(wg[:], w_gate.rearrange("(k p) e -> p k e", p=P)).then_inc(s_small, 16)
            eng.dma_start(bg[:], b_gate.partition_broadcast(P)).then_inc(s_small, 16)

            def x_hi(t, p, h):
                c_t1.wait(eng, t)
                c_mm.wait(eng, t - 2)
                c_xhi.done(eng.activation(xT[:, p, HI, :, :], psT[:, 0, :, :], ACT.Copy))

            def norm1(t, p, h):
                c_rs[0].wait(eng, t)
                c_ln1.done(eng.activation(xb[:, p, :], xb[:, p, :], ACT.Identity, bias=rs[:, 0, 2:3], scale=rs[:, 0, 1:2]))

            def norm2(t, p, h):
                l_x2.wait(eng, p, h - 1)
                c_rs[1].wait(eng, t)
                c_ln2.done(eng.activation(x2[:, p, :], xr[:, p, :], ACT.Identity, bias=rs[:, 1, 2:3], scale=rs[:, 1, 1:2]))

            def copy_gated(t, p, h):
                c_gate.wait(eng, t)
                c_logit.wait(eng, t - 1)
                c_gated.done(eng.activation(gated[:], psG[0:4 * N_EXP, 0:P], ACT.Copy))

            def piece_hi(t, p, h):
                l_raw0.wait(eng, p, h)
                c_hi0.done(eng.activation(slots[:, 0, HI, bass.ds(h, 1), p * HALF:(p + 1) * HALF].rearrange("p a n -> p (a n)"),
                                          raw[:, p, 0:HALF], ACT.Copy))

            norm1(0, 0, 0)
            for r in range(NT):
                c_wt.wait(eng, r)
                c_whi.done(eng.activation(wT[:, HI, :, r * P:(r + 1) * P], psT[:, w_half_of(r), :, :], ACT.Copy))
                if r == 0:
                    x_hi(0, 0, 0)
                if r == X1_AT:
                    norm1(1, 1, 0)
            c_fold.wait(eng, 0)
            eng.activation(foldedT[:, 0, :], psF[0], ACT.Copy)
            c_fold_read.done(eng.activation(foldedT[:, 1, :], psF[1], ACT.Copy))
            pipeline(eng, [(x_hi, 1, 1), (norm2, -1), (norm1, 2, 2), (piece_hi, 0), (copy_gated, 0)], NB)

            def rows_hi(b, p, h):
                c_turn.wait(eng, b)
                c_half.wait(eng, b - 2)
                hi = eng.activation(xT[:, p, HI, :, :], psT[:, p, :, :], ACT.Copy)
                if isinstance(b, int) and b == 0:
                    hi.then_inc(c_rhi.sem, 2)
                    return
                c_rhi.done(hi)
                c_rlo.wait(eng, b - 1)
                c_rhi.done(eng.activation(x2T[:], psT[:, p, :, :], ACT.Copy))

            def seed_half(b, slot, n):
                cols = slice(n * HALF, (n + 1) * HALF)
                c_out.wait(eng, b - 1, n + 1)
                c_seed.done(eng.activation(psO[:, n, :], bias_slot[:, bass.ds(slot, 1), cols].rearrange("p a n -> p (a n)"),
                                           ACT.Copy))

            def biases_of(b):
                slot = eng.value_load(slot_of[0:1, bass.ds(b, 1)], min_val=0, max_val=1)
                ready = eng.value_load(ready_of[0:1, bass.ds(b, 1)], min_val=2 * KT, max_val=2 * KT * N_EXP)
                eng.wait_ge(c_split.sem, ready)
                return slot

            def relu_and_seed(b, p, h):
                l_add.wait(eng, p, h - 1)
                last = isinstance(b, int) and b == N_BLOCKS - 1
                for n in range(NH):
                    c_half.wait(eng, b, n + 1)
                    c_out.done(eng.activation(xb[:, p, n * HALF:(n + 1) * HALF], psO[:, n, :], ACT.Relu, scale=1.0 / TOP_K))
                    if not last:
                        if n == 0:
                            slot = biases_of(b + 1)
                        seed_half(b + 1, slot, n)

            c_mm.wait(eng, NB - 1)
            c_res.wait(eng, NB - 1)
            c_tab_d.wait(eng, 0, 14)
            l_bias.wait(eng, 0, 0)
            slot = biases_of(0)
            for n in range(NH):
                seed_half(0, slot, n)
            pipeline(eng, [(rows_hi, 1), (relu_and_seed, 0)], N_BLOCKS)

        @block.vector
        def _(eng):
            eng.wait_ge(s_const, NCONST)
            s_vconst.done(eng.memset(count[:], 0.0))
            s_vconst.done(eng.memset(queue[:], 0.0))
            s_vconst.done(eng.tensor_reduce(eminus[:, 0:1], upto[:], AX.X, ALU.add))
            s_vconst.wait(eng, 2)
            s_vconst.done(eng.tensor_scalar(eminus[:, 1:2], eminus[:, 0:1], -1.0, 1.0, ALU.mult, ALU.add))

            def stats(c, src, which, t, p, landed):
                landed()
                c.wait(eng, t - 1)
                for g in range(2):
                    c.done(eng.bn_stats(st[:, which, g, :], src[:, g * HD:(g + 1) * HD]))
                c.wait(eng, t, 2, alone=s_void)
                c.done(eng.bn_aggr(mv[:, which, p, :], st[:, which, :, :].rearrange("p g s -> p (g s)")))

            def stats1(t, p, h):
                def landed():
                    l_x.wait(eng, p, h)
                    c_rs[0].wait(eng, t - 2)
                    c_ln1.wait(eng, t - 2)
                stats(c_st1, xb[:, p, :], 0, t, p, landed)

            def stats2(t, p, h):
                def landed():
                    c_res.wait(eng, t)
                    c_rs[1].wait(eng, t - 2)
                stats(c_st2, xr[:, p, :], 1, t, p, landed)

            def x_lo(t, p, h):
                c_xhi.wait(eng, t)
                c_xlo.done(eng.tensor_tensor(xT[:, p, LO, :, :], psT[:, 0, :, :], xT[:, p, HI, :, :].bitcast(F32), ALU.subtract))

            def residual_half(n):
                cols = slice(n * HALF, (n + 1) * HALF)

                def residual(t, p, h):
                    if n == 0:
                        l_xr.wait(eng, p, h)
                    c_mm.wait(eng, t, n + 1)
                    c_res.done(eng.tensor_tensor(xr[:, p, cols], xr[:, p, cols], psO[:, n, :], ALU.add))
                return residual

            def top2(t, p, h):
                c_logit.wait(eng, t)
                c_top.wait(eng, t - 1)
                std = kept[:, bass.ds(t, 1), 0:1].rearrange("p a b -> p (a b)").to_broadcast([P, N_EXP])
                c_top.done(eng.tensor_tensor(share[:], psL[:, 0:N_EXP], std, ALU.mult))
                c_top.wait(eng, t, 1)
                c_top.done(eng.tensor_tensor(logit[:], share[:], psL[:, N_EXP:2 * N_EXP], ALU.add))
                c_top.wait(eng, t, 2)
                c_rs[1].wait(eng, t, 2)
                c_top.done(eng.scalar_tensor_tensor(share[:], wg_sum[:], rs[:, 1, 3:4], logit[:], ALU.mult, ALU.add))
                c_top.wait(eng, t, 3)
                c_rs[1].wait(eng, t, 3)
                c_top.done(eng.scalar_tensor_tensor(logit[:], share[:], rs[:, 1, 1:2], bg[:], ALU.mult, ALU.add))
                c_top.wait(eng, t, 4)
                mine = logit[:].unsqueeze(2).to_broadcast([P, N_EXP, N_EXP])
                other = logit[:].unsqueeze(1).to_broadcast([P, N_EXP, N_EXP])
                c_top.done(eng.tensor_tensor(eq[:], other, mine, ALU.is_equal))
                c_top.done(eng.tensor_tensor(gt[:], other, mine, ALU.is_gt))
                c_top.wait(eng, t, 5)
                c_top.done(eng.tensor_tensor(eq[:], eq[:], tri_e[:], ALU.mult))
                c_top.wait(eng, t, 7)
                c_top.done(eng.tensor_tensor(gt[:], gt[:], eq[:], ALU.add))
                c_top.wait(eng, t, 8)
                c_top.done(eng.tensor_reduce(rank[:], gt[:], AX.X, ALU.add))
                c_top.wait(eng, t, 9)
                c_pos.wait(eng, t - 1)
                c_hot.wait(eng, t - 2)
                c_top.done(eng.tensor_scalar(chosen[:], rank[:], float(TOP_K), None, ALU.is_lt))
                c_top.done(eng.tensor_scalar(chosen_tok[:, p, :], rank[:], float(TOP_K), tok[:, 0:1], ALU.is_lt, ALU.mult))
                c_top.wait(eng, t, 11)
                c_top.done(eng.tensor_scalar(tok[:], tok[:], float(P), None, ALU.add))

            def one_hots(t, p, h):
                c_pos.wait(eng, t)
                c_hot.wait(eng, t - 1)
                c_hot.done(eng.tensor_tensor(pos[:], psN[:, 0, :], count[:], ALU.add))
                c_hot.wait(eng, t, 1)
                c_hot.done(eng.tensor_tensor(count[:], count[:], psN[:, 1, :], ALU.add))
                c_hot.done(eng.tensor_copy(pos_i[:], pos[:]))
                c_hot.wait(eng, t, 3)
                c_hot.done(eng.tensor_scalar(pos_r[:], pos_i[:], P - 1, None, ALU.bitwise_and))
                c_hot.done(eng.tensor_scalar(pos_j[:], pos_i[:], P.bit_length() - 1, None, ALU.logical_shift_right))
                c_hot.wait(eng, t, 5)
                c_ids.wait(eng, t - 1)
                c_hot.done(eng.tensor_tensor(blk_hot[:], lane[:, 0:JB].unsqueeze(1).to_broadcast([P, N_EXP, JB]),
                                             pos_j[:].unsqueeze(2).to_broadcast([P, N_EXP, JB]), ALU.is_equal))
                c_hot.done(eng.tensor_tensor(row_hot[:], lane[:].unsqueeze(1).to_broadcast([P, N_EXP, P]),
                                             pos_r[:].unsqueeze(2).to_broadcast([P, N_EXP, P]), ALU.is_equal))
                c_hot.wait(eng, t, 6)
                c_hot.done(eng.tensor_tensor(blk_tok[:], blk_hot[:],
                                             chosen_tok[:, p, :].unsqueeze(2).to_broadcast([P, N_EXP, JB]), ALU.mult))

            def add_queue(t, p, h):
                c_ids.wait(eng, t)
                c_queue.wait(eng, t - 1)
                c_queue.done(eng.tensor_tensor(queue[:], queue[:], psQ, ALU.add))

            def split_chunk(e_slot, kt, q):
                l_raw.wait(eng, kt % 2, q)
                c = KT + 2 * q + kt % 2
                c_split.done(eng.tensor_copy(slots[:, e_slot, HI, kt, :], raw[:, kt % 2, :]))
                c_split.wait(eng, c, 1)
                c_split.done(eng.tensor_tensor(slots[:, e_slot, LO, kt, :], raw[:, kt % 2, :],
                                               slots[:, e_slot, HI, kt, :].bitcast(F32), ALU.subtract))

            def split_expert(e_slot, e_half, q0, from_chunk=0):
                for kt in range(from_chunk, KT):
                    if kt == KT - 1:
                        l_bias.wait(eng, e_slot, e_half)
                    split_chunk(e_slot, kt, q0 + kt // 2)

            c_prep.done(eng.tensor_tensor(fold[:], ident[0:4 * N_EXP, 0:2 * N_EXP], ident[0:4 * N_EXP, 2 * N_EXP:4 * N_EXP], ALU.add))

            def sum_mask(r):
                eng.wait_ge(s_m[r], 16)
                c_msum.done(eng.tensor_reduce(msum[:, r, :], mask_stage[:, r, :].rearrange("p (g s) -> p g s", s=SUB),
                                              AX.X, ALU.add))

            def w_lo(r):
                c_whi.wait(eng, r)
                here = slice(r * P, (r + 1) * P)
                c_wlo.done(eng.tensor_tensor(wT[:, LO, :, here], psT[:, w_half_of(r), :, :], wT[:, HI, :, here].bitcast(F32), ALU.subtract))

            def element_mask(r):
                c_group.wait(eng, r)
                c_em.done(eng.tensor_scalar(emask[:, r, :], psG[:, 0:NSUB], 0.0, None, ALU.is_gt))

            sum_mask(0)
            element_mask(0)
            for r in range(NT):
                for t in range(2):
                    if r == t * X1_AT:
                        stats1(t, t, 0)
                if r + 1 < NT:
                    sum_mask(r + 1)
                if r > 0:
                    element_mask(r)
                if r == 1:
                    w_lo(0)
                elif r == 2:
                    x_lo(0, 0, 0)
                elif r > 2:
                    w_lo(r - 2)
                if r == 3:
                    eng.wait_ge(s_small, 32)
                    c_part.done(eng.tensor_reduce(wg_part[:], wg[:].rearrange("p k e -> p e k"), AX.X, ALU.add))
            w_lo(NT - 2)
            w_lo(NT - 1)
            c_unfold.wait(eng, 0)
            folded = psU.rearrange("p (k e) -> p k e", e=N_EXP)
            c_gw.done(eng.tensor_copy(gates[:, :, HI, 0, :], wg[:]))
            c_gw.done(eng.tensor_copy(gates[:, :, HI, 1, :], folded))
            c_gw.done(eng.tensor_copy(wg_sum[:], psW))
            c_gw.wait(eng, 0, 2)
            c_gw.done(eng.tensor_tensor(gates[:, :, LO, 0, :], wg[:], gates[:, :, HI, 0, :].bitcast(F32), ALU.subtract))
            c_gw.done(eng.tensor_tensor(gates[:, :, LO, 1, :], folded, gates[:, :, HI, 1, :].bitcast(F32), ALU.subtract))
            pipeline(eng, [(residual_half(1), -1), (stats2, -1), (stats1, 2, 2), (top2, -1), (x_lo, 1, 1),
                           (residual_half(0), 0), (add_queue, -2, 0, NB - 1), (one_hots, -1)], NB)

            c_hot.wait(eng, NB - 1, 2)
            for p in range(2):
                l_x1.wait(eng, p, NB // 2 - 1)
            c_ln2.wait(eng, NB - 1)
            tab = c_tab_d
            tab.done(eng.tensor_tensor(act_row[:], count[:].unsqueeze(2).to_broadcast([P, N_EXP, JB]),
                                       lane_first[:].unsqueeze(1).to_broadcast([P, N_EXP, JB]), ALU.is_gt))
            add_queue(NB - 1, 1, NB // 2 - 1)
            c_tab_p.wait(eng, 0, 1)
            tab.done(eng.tensor_copy(act_col[:, 0:1], psG[:, 0:1]))
            tab.done(eng.tensor_copy(act_c16[:, 0:1], psG[:, 0:1]))
            c_tab_p.wait(eng, 0, 2)
            tab.done(eng.tensor_copy(queueT[:], psT[:, 0, 0, :]))
            c_tab_p.wait(eng, 0, 3)
            tab.done(eng.tensor_copy(act_col[:, 1:2], psG[:, 16:17]))
            tab.wait(eng, 0, 5)
            tab.done(eng.tensor_scalar(pick[:], lane[:, 0:N_BLOCKS], act_col[:, 1:2], act_col[:, 0:1], ALU.is_equal, ALU.mult))
            tab.done(eng.tensor_scalar(meta_in[:, N_BLOCKS:], upto[:], act_col[:, 0:1], None, ALU.mult))
            tab.wait(eng, 0, 6)
            tab.done(eng.tensor_scalar(meta_in[:, 0:N_BLOCKS], pick[:], eminus[:, 1:2], None, ALU.mult))
            c_tab_p.wait(eng, 0, 4)
            tab.done(eng.tensor_scalar(empty[:], psG[:, 64:64 + N_BLOCKS], 0.0, spare[:, 0:1], ALU.is_equal, ALU.mult))
            tab.done(eng.tensor_scalar(e_of[:], psG[:, 128:128 + N_BLOCKS], float(N_EXP - 1), None, ALU.add))
            tab.done(eng.tensor_scalar(through[:], psG[:, 128 + N_BLOCKS:128 + N_BLOCKS + N_EXP], float(NH), float(NH), ALU.mult, ALU.add))
            tab.wait(eng, 0, 10)
            tab.done(eng.scalar_tensor_tensor(tok_of[:], psG[:, 64:64 + N_BLOCKS], -1.0, empty[:], ALU.add, ALU.add))
            tab.done(eng.tensor_scalar(slot_of[:], e_of[:], 1, None, ALU.bitwise_and))
            tab.done(eng.tensor_scalar(ready_of[:], e_of[:], 1.0, float(2 * KT), ALU.add, ALU.mult))

            c_mm.wait(eng, NB - 1)
            for kt in range(2):
                split_chunk(1, kt, 0)
            c_rhi.wait(eng, 0)
            c_rlo.done(eng.tensor_tensor(xT[:, 0, LO, :, :], psT[:, 0, :, :], xT[:, 0, HI, :, :].bitcast(F32), ALU.subtract))
            split_expert(1, 0, 0, 2)
            tab.wait(eng, 0, 14)
            with eng.Fori(1, N_EXP // 2) as g:
                for s in range(2):
                    used = eng.value_load(through[0:1, bass.ds(2 * g + s - 2, 1)], min_val=NH, max_val=NH * (N_BLOCKS + 1))
                    eng.wait_ge(c_half.sem, used)
                    split_expert(s, g, KT * g + (s - 1) * KT // 2)

        @block.gpsimd
        def _(eng):
            def const(instruction):
                instruction.then_inc(s_const, 1)

            const(eng.memset(ident[:], 0.0))
            const(eng.memset(group[:], 1.0))
            const(eng.memset(tri[:], 1.0))
            const(eng.memset(ones16[:], 1.0))
            const(eng.memset(ones[:], 1.0))
            const(eng.memset(tri_e[:], 1.0))
            const(eng.memset(upto[:], 1.0))
            const(eng.memset(raw[:, 0, :], 0.0))
            const(eng.memset(half_neg[:], -0.5))
            eng.memset(rs[:], 0.0).then_inc(c_split.sem, 2 * KT)
            const(eng.iota(lane[:], [[1, P]], base=0, channel_multiplier=0, allow_small_or_imprecise_dtypes=True))
            const(eng.iota(lane_first[:], [[P, JB]], base=0, channel_multiplier=0, allow_small_or_imprecise_dtypes=True))
            const(eng.iota(tok[:], [[0, 1]], base=1, channel_multiplier=1, allow_small_or_imprecise_dtypes=True))
            eng.wait_ge(s_const, 12)
            const(eng.iota(spare[:], [[0, 1]], base=N_TOK + 1, channel_multiplier=1, allow_small_or_imprecise_dtypes=True))
            const(eng.affine_select(out=ident[:], in_=ident[:], pattern=[[-1, P]], compare_op=ALU.not_equal, fill=1.0,
                                    base=0, channel_multiplier=1))
            g4 = group[:].rearrange("p (g s) -> p g s", s=SUB)
            const(eng.affine_select(out=g4, in_=g4, pattern=[[-SUB, P // SUB], [0, SUB]], compare_op=ALU.is_ge, fill=0.0,
                                    base=0, channel_multiplier=1))
            const(eng.affine_select(out=tri[:], in_=tri[:], pattern=[[1, P]], compare_op=ALU.is_ge, fill=0.0,
                                    base=-1, channel_multiplier=-1))
            const(eng.affine_select(out=tri_e[:], in_=tri_e[:], pattern=[[1, N_EXP], [-1, N_EXP]], compare_op=ALU.is_ge,
                                    fill=0.0, base=-1, channel_multiplier=0))
            const(eng.affine_select(out=upto[:], in_=upto[:], pattern=[[JB, N_EXP]], compare_op=ALU.is_ge, fill=0.0,
                                    base=JB - 1, channel_multiplier=-1))
            eng.wait_ge(s_const, 18)
            const(eng.affine_select(out=g4, in_=g4, pattern=[[SUB, P // SUB], [0, SUB]], compare_op=ALU.is_ge, fill=0.0,
                                    base=SUB - 1, channel_multiplier=-1))

            def inverse_std(which, stats_done):
                c = c_rs[which]

                def run(t, p, h):
                    c.wait(eng, t - 1)
                    if which == 0:
                        c_ln1.wait(eng, t - 1)
                    else:
                        c_ln2.wait(eng, t - 1)
                        c_top.wait(eng, t - 1, 4, alone=s_void)
                    stats_done.wait(eng, t, alone=s_void)
                    mean, var = mv[:, which, p, 0:1], mv[:, which, p, 1:2]
                    std2, inverse, shift, drop = (rs[:, which, i:i + 1] for i in range(4))
                    kept_std, kept_mean = (kept[:, bass.ds(t, 1), i:i + 1].rearrange("p a b -> p (a b)") for i in range(2))
                    c.done(eng.tensor_scalar(std2, var, EPS, None, ALU.add))
                    if which == 0:
                        c.done(eng.tensor_copy(kept_mean, mean))
                    else:
                        c.done(eng.tensor_tensor(drop, kept_mean, mean, ALU.subtract))
                    c.wait(eng, t, 1)
                    c.done(eng.tensor_tensor(inverse, std2, half_neg[:], ALU.pow))
                    c.wait(eng, t, 3, alone=s_void)
                    c.done(eng.tensor_scalar(shift, mean, inverse, -1.0, ALU.mult, ALU.mult))
                    if which == 0:
                        c.done(eng.tensor_tensor(kept_std, std2, inverse, ALU.mult))
                return run

            def piece_lo(t, p, h):
                c_hi0.wait(eng, t)
                cols = slice(p * HALF, (p + 1) * HALF)
                c_lo0.done(eng.tensor_tensor(slots[:, 0, LO, bass.ds(h, 1), cols].rearrange("p a n -> p (a n)"), raw[:, p, 0:HALF],
                                             slots[:, 0, HI, bass.ds(h, 1), cols].rearrange("p a n -> p (a n)").bitcast(F32), ALU.subtract))

            for r in range(NT):
                c_em.wait(eng, r)
                eng.wait_ge(s_w[r], 16)
                rows = w_stage[:, r, :].rearrange("p (g s) -> p g s", s=SUB)
                c_wm.done(eng.tensor_tensor(rows, rows, emask[:, r, :].unsqueeze(2).to_broadcast([P, NSUB, SUB]), ALU.mult))
                for t in range(2):
                    if r == t * X1_AT:
                        inverse_std(0, c_st1)(t, t, 0)
            c_fold.wait(eng, 0)
            pipeline(eng, [(inverse_std(1, c_st2), -1), (inverse_std(0, c_st1), 2, 2), (piece_lo, 0)], NB)

            def set_tokens(which, b, p):
                c_tok[which].done(eng.tensor_copy(tok_at[:, which, p:p + 1], tok_of[:, bass.ds(b, 1)]))
                c_tok[which].wait(eng, b, alone=s_void)

            def by_token(which, p):
                return bass.IndirectOffsetOnAxis(ap=tok_at[:, which, p:p + 1], axis=0)

            def gather_rows(b, p, h):
                c_turn.wait(eng, b - 2)
                set_tokens(GATHER, b, p)
                l_gather.done(eng.indirect_dma_start(x2[:, p, :], None, x2_rows, by_token(GATHER, p),
                                                     bounds_check=N_TOK - 1, oob_is_err=False), p)

            def rows_lo(b, p, h):
                c_rhi.wait(eng, b)
                c_rlo.done(eng.tensor_tensor(xT[:, p, LO, :, :], x2T[:], xT[:, p, HI, :, :].bitcast(F32), ALU.subtract))

            def add_rows(b, p, h):
                if isinstance(b, int):
                    if b > 0:
                        l_add.wait(eng, 1 - p, (b - 1) // 2)
                else:
                    l_add.wait(eng, 1 - p, h if p == 1 else h - 1)
                set_tokens(ADD, b, p)
                c_out.wait(eng, b, alone=s_void)
                l_add.done(eng.indirect_dma_start(out, by_token(ADD, p), xb[:, p, :], None, bounds_check=N_TOK + P - 1,
                                                  compute_op=ALU.add), p)

            for p in range(2):
                l_x1.wait(eng, p, NB // 2 - 1)
                l_x2.wait(eng, p, NB // 2 - 1)
            eng.wait_ge(s_spare, 16)
            c_tab_d.wait(eng, 0, 12)
            pipeline(eng, [(gather_rows, 2), (rows_lo, 1, 1), (add_rows, 0)], N_BLOCKS)
            for p in range(2):
                l_add.wait(eng, p, (N_BLOCKS - 1 - p) // 2)


_INS = ["L0_attn_data", "L0_attn_weight", "L0_attn_mask", "L0_ffn_W_gate", "L0_ffn_b_gate", "L0_ffn_W_e", "L0_ffn_b_e"]


def kernel(**inputs):
    import numpy as np
    import concourse.bacc as bacc
    from concourse.bass_utils import run_bass_kernel_spmd

    nc = bacc.Bacc("TRN2", target_bir_lowering=False, num_devices=1)
    B, S, D = inputs["L0_attn_data"].shape
    arrays, args = {}, []
    for name in _INS:
        a = np.ascontiguousarray(inputs[name])
        if name == "L0_attn_data":
            a = a.reshape(B * S, D)
        arrays[name] = a
        args.append(nc.dram_tensor(name, a.shape, mybir.dt.from_np(a.dtype), kind="ExternalInput").ap())
    args.append(nc.dram_tensor("rows_out", (B * S + P, D), F32, kind="ExternalOutput").ap())
    build(nc, *args)
    r = run_bass_kernel_spmd(nc, [arrays], core_ids=[0])
    return r.results[0]["rows_out"][:B * S].reshape(B, S, D)
```
